# Optimizing a Trainium2 kernel written in Bass

```python
import numpy as np
import jax
import jax.numpy as jnp

def _softmax(x, axis=-1):
    return jax.nn.softmax(x, axis=axis)

def _gelu(x):
    return jax.nn.gelu(x, approximate=True)

def _silu(x):
    return jax.nn.silu(x)

def _sigmoid(x):
    return jax.nn.sigmoid(x)

def _layernorm(x, axis=-1, eps=1e-05):
    m = jnp.mean(x, axis=axis, keepdims=True)
    v = jnp.var(x, axis=axis, keepdims=True)
    return (x - m) / jnp.sqrt(v + eps)

def _scatter_add(tgt, idx, src, axis=0):
    return tgt.at[idx].add(src)

def _segment_sum(src, seg, n):
    return jax.ops.segment_sum(src, seg, n)
kernel_name = 'mk_lm_tower_d1_tok_ids1024_r4_05e1aa'

def setup_inputs(seed: int=0):
    np.random.seed(seed)
    _w = jnp.asarray

    def _rec_inputs():
        import jax
        import jax.numpy as jnp
        _rk = jax.random.key(seed)
        x = jax.random.randint(jax.random.fold_in(_rk, 1), (64, 128), 0, 12564, jnp.int32)
        return x
    x = _rec_inputs()

    def _L0_tok_setup():
        import jax, jax.numpy as jnp
        import numpy as np
        B, T, D, INNER, N, V, L, P = (4, 1024, 256, 512, 64, 50257, 4, 5000)
        DECAY, INP = (0.95, 0.05)

        def _silu(x):
            return x * jax.nn.sigmoid(x)

        def _layer(x, W_in_l, cw, cb, WB, WC, Dv, Wo, g, b):
            xp = x @ W_in_l.T
            x_in, x_gate = jnp.split(xp, 2, axis=-1)
            xc = jnp.transpose(x_in, (0, 2, 1))
            xc = jnp.pad(xc, ((0, 0), (0, 0), (3, 0)))
            xc = jax.lax.conv_general_dilated(xc, cw, window_strides=(1,), padding='VALID', dimension_numbers=('NCH', 'OIH', 'NCH'), feature_group_count=INNER)
            xc = xc + cb[None, :, None]
            u = _silu(jnp.transpose(xc, (0, 2, 1)))
            Bu = u @ WB.T

            def step(h, bu):
                h = DECAY * h + INP * bu
                return (h, h)
            h0 = jnp.zeros((x.shape[0], Bu.shape[-1]), x.dtype)
            _, hs = jax.lax.scan(step, h0, jnp.swapaxes(Bu, 0, 1))
            hs = jnp.swapaxes(hs, 0, 1)
            y = hs @ WC.T + Dv * u
            y = y * _silu(x_gate)
            y = y @ Wo.T
            z = y + x
            mu = jnp.mean(z, axis=-1, keepdims=True)
            var = jnp.var(z, axis=-1, keepdims=True)
            return (z - mu) * jax.lax.rsqrt(var + 1e-05) * g + b
        key = jax.random.key(seed)
        ks = jax.random.split(key, 10)
        s = 0.02
        return {'tokens': jax.random.randint(ks[0], (B, T), 0, V), 'tok_emb': jax.random.normal(ks[1], (V, D), jnp.float32) * s, 'pos_emb': jax.random.normal(ks[2], (P, D), jnp.float32) * s, 'W_in': jax.random.normal(ks[3], (L, 2 * INNER, D), jnp.float32) * s, 'conv_w': jax.random.normal(ks[4], (L, INNER, 1, 4), jnp.float32) * s, 'conv_b': jnp.zeros((L, INNER), jnp.float32), 'W_B': jax.random.normal(ks[5], (L, N, INNER), jnp.float32) * s, 'W_C': jax.random.normal(ks[6], (L, INNER, N), jnp.float32) * s, 'D_vec': jax.random.normal(ks[7], (L, INNER), jnp.float32) * s, 'W_out': jax.random.normal(ks[8], (L, D, INNER), jnp.float32) * s, 'ln_g': jnp.ones((L, D), jnp.float32), 'ln_b': jnp.zeros((L, D), jnp.float32)}
    _L0_tok_all = _L0_tok_setup()
    _L0_tok_in = {k: v for k, v in _L0_tok_all.items() if k in ('tok_emb', 'pos_emb', 'W_in', 'conv_w', 'conv_b', 'W_B', 'W_C', 'D_vec', 'W_out', 'ln_g', 'ln_b')}
    del _L0_tok_all

    def _L0_attn_setup():
        import jax, jax.numpy as jnp
        import numpy as np
        D_K, HEADS, K_BITS, L_TABLES = (256, 16, 4, 8)
        HEAD_DIM = D_K // HEADS
        R = 1 << K_BITS
        S = L_TABLES * R
        B, T = (4, 1024)

        def _protos_T():
            r = np.arange(R)
            bits = r[:, None] >> K_BITS - 1 - np.arange(K_BITS) & 1
            corners = (2.0 * bits - 1.0).astype(np.float32)
            return jnp.asarray(corners.T)
        key = jax.random.key(seed)
        ks = jax.random.split(key, 7)
        x = jax.random.normal(ks[0], (B, T, D_K), dtype=jnp.float32)
        sc = 0.02
        Wq = jax.random.normal(ks[1], (D_K, D_K), dtype=jnp.float32) * sc
        Wk = jax.random.normal(ks[2], (D_K, D_K), dtype=jnp.float32) * sc
        Wv = jax.random.normal(ks[3], (D_K, D_K), dtype=jnp.float32) * sc
        Wo = jax.random.normal(ks[4], (D_K, D_K), dtype=jnp.float32) * sc
        bo = jnp.zeros((D_K,), dtype=jnp.float32)
        planes = jax.random.normal(ks[5], (L_TABLES * K_BITS, HEAD_DIM), dtype=jnp.float32)
        planes_T = planes.T
        logit_temp = jnp.zeros((), dtype=jnp.float32)
        protos_T = _protos_T()
        return {'x': x, 'Wq': Wq, 'Wk': Wk, 'Wv': Wv, 'Wo': Wo, 'bo': bo, 'planes_T': planes_T, 'protos_T': protos_T, 'logit_temp': logit_temp}
    _L0_attn_all = _L0_attn_setup()
    _L0_attn_in = {k: v for k, v in _L0_attn_all.items() if k in ('Wq', 'Wk', 'Wv', 'Wo', 'bo', 'planes_T', 'protos_T', 'logit_temp')}
    del _L0_attn_all

    def _L0_ffn_setup():
        import jax, jax.numpy as jnp
        import numpy as np
        FP8_MAX = 448.0
        key = jax.random.key(seed)
        k_x, k_w, k_b = jax.random.split(key, 3)
        B, S, IN, OUT = (4, 2048, 256, 256)
        x = jax.random.normal(k_x, (B, S, IN), dtype=jnp.float32)
        w_fp32 = jax.random.normal(k_w, (OUT, IN), dtype=jnp.float32)
        weight_fp8 = w_fp32.astype(jnp.float8_e4m3fn).astype(jnp.float32)
        bias = jax.random.normal(k_b, (OUT,), dtype=jnp.float32)
        input_scale = jnp.ones((1,), dtype=jnp.float32)
        weight_scale = jnp.ones((1,), dtype=jnp.float32)
        return {'x': x, 'weight_fp8': weight_fp8, 'bias': bias, 'input_scale': input_scale, 'weight_scale': weight_scale}
    _L0_ffn_all = _L0_ffn_setup()
    _L0_ffn_in = {k: v for k, v in _L0_ffn_all.items() if k in ('weight_fp8', 'bias', 'input_scale', 'weight_scale')}
    del _L0_ffn_all
    return {'x': x, 'L0_tok_tok_emb': _L0_tok_in['tok_emb'], 'L0_tok_pos_emb': _L0_tok_in['pos_emb'], 'L0_tok_W_in': _L0_tok_in['W_in'], 'L0_tok_conv_w': _L0_tok_in['conv_w'], 'L0_tok_conv_b': _L0_tok_in['conv_b'], 'L0_tok_W_B': _L0_tok_in['W_B'], 'L0_tok_W_C': _L0_tok_in['W_C'], 'L0_tok_D_vec': _L0_tok_in['D_vec'], 'L0_tok_W_out': _L0_tok_in['W_out'], 'L0_tok_ln_g': _L0_tok_in['ln_g'], 'L0_tok_ln_b': _L0_tok_in['ln_b'], 'L0_attn_Wq': _L0_attn_in['Wq'], 'L0_attn_Wk': _L0_attn_in['Wk'], 'L0_attn_Wv': _L0_attn_in['Wv'], 'L0_attn_Wo': _L0_attn_in['Wo'], 'L0_attn_bo': _L0_attn_in['bo'], 'L0_attn_planes_T': _L0_attn_in['planes_T'], 'L0_attn_protos_T': _L0_attn_in['protos_T'], 'L0_attn_logit_temp': _L0_attn_in['logit_temp'], 'L0_ffn_weight_fp8': _L0_ffn_in['weight_fp8'], 'L0_ffn_bias': _L0_ffn_in['bias'], 'L0_ffn_input_scale': _L0_ffn_in['input_scale'], 'L0_ffn_weight_scale': _L0_ffn_in['weight_scale']}

def reference(x, L0_tok_tok_emb, L0_tok_pos_emb, L0_tok_W_in, L0_tok_conv_w, L0_tok_conv_b, L0_tok_W_B, L0_tok_W_C, L0_tok_D_vec, L0_tok_W_out, L0_tok_ln_g, L0_tok_ln_b, L0_attn_Wq, L0_attn_Wk, L0_attn_Wv, L0_attn_Wo, L0_attn_bo, L0_attn_planes_T, L0_attn_protos_T, L0_attn_logit_temp, L0_ffn_weight_fp8, L0_ffn_bias, L0_ffn_input_scale, L0_ffn_weight_scale):
    import jax
    import jax.numpy as jnp

    def _L0_tok_ref(tokens, tok_emb, pos_emb, W_in, conv_w, conv_b, W_B, W_C, D_vec, W_out, ln_g, ln_b):
        import jax, jax.numpy as jnp
        import numpy as np
        B, T, D, INNER, N, V, L, P = (4, 1024, 256, 512, 64, 50257, 4, 5000)
        DECAY, INP = (0.95, 0.05)

        def _silu(x):
            return x * jax.nn.sigmoid(x)

        def _layer(x, W_in_l, cw, cb, WB, WC, Dv, Wo, g, b):
            xp = x @ W_in_l.T
            x_in, x_gate = jnp.split(xp, 2, axis=-1)
            xc = jnp.transpose(x_in, (0, 2, 1))
            xc = jnp.pad(xc, ((0, 0), (0, 0), (3, 0)))
            xc = jax.lax.conv_general_dilated(xc, cw, window_strides=(1,), padding='VALID', dimension_numbers=('NCH', 'OIH', 'NCH'), feature_group_count=INNER)
            xc = xc + cb[None, :, None]
            u = _silu(jnp.transpose(xc, (0, 2, 1)))
            Bu = u @ WB.T

            def step(h, bu):
                h = DECAY * h + INP * bu
                return (h, h)
            h0 = jnp.zeros((x.shape[0], Bu.shape[-1]), x.dtype)
            _, hs = jax.lax.scan(step, h0, jnp.swapaxes(Bu, 0, 1))
            hs = jnp.swapaxes(hs, 0, 1)
            y = hs @ WC.T + Dv * u
            y = y * _silu(x_gate)
            y = y @ Wo.T
            z = y + x
            mu = jnp.mean(z, axis=-1, keepdims=True)
            var = jnp.var(z, axis=-1, keepdims=True)
            return (z - mu) * jax.lax.rsqrt(var + 1e-05) * g + b
        x = tok_emb[tokens] + pos_emb[jnp.arange(tokens.shape[1])][None]
        for l in range(L):
            x = _layer(x, W_in[l], conv_w[l], conv_b[l], W_B[l], W_C[l], D_vec[l], W_out[l], ln_g[l], ln_b[l])
        return x

    def _L0_attn_ref(x, Wq, Wk, Wv, Wo, bo, planes_T, protos_T, logit_temp):
        import jax, jax.numpy as jnp
        import numpy as np
        D_K, HEADS, K_BITS, L_TABLES = (256, 16, 4, 8)
        HEAD_DIM = D_K // HEADS
        R = 1 << K_BITS
        S = L_TABLES * R
        B, T = (4, 1024)

        def _protos_T():
            r = np.arange(R)
            bits = r[:, None] >> K_BITS - 1 - np.arange(K_BITS) & 1
            corners = (2.0 * bits - 1.0).astype(np.float32)
            return jnp.asarray(corners.T)
        Bx, Tx, D = x.shape
        dim = planes_T.shape[0]
        H = D // dim
        k_bits, r = protos_T.shape
        l_tables = planes_T.shape[1] // k_bits
        s = l_tables * r

        def heads(W):
            return (x @ W.T).reshape(Bx, Tx, H, dim).transpose(0, 2, 1, 3)
        Q, K, V = (heads(Wq), heads(Wk), heads(Wv))
        scale = jnp.clip(jnp.exp(logit_temp), 0.01, 20.0)
        projK = jnp.einsum('bhtd,dp->bhtp', K, planes_T).reshape(Bx, H, Tx, l_tables, k_bits)
        logitsK = jnp.einsum('bhtlk,kr->bhtlr', jnp.tanh(projK) / scale, protos_T)
        probsK = jax.nn.softmax(logitsK, axis=-1).reshape(Bx, H, Tx, s)
        bucket_K = jnp.einsum('bhts,bhtd->bhsd', probsK, K)
        bucket_V = jnp.einsum('bhts,bhtd->bhsd', probsK, V)
        scores = jnp.einsum('bhtd,bhsd->bhts', Q, bucket_K) / jnp.sqrt(jnp.float32(dim))
        attn = jax.nn.softmax(scores, axis=-1)
        out = jnp.einsum('bhts,bhsd->bhtd', attn, bucket_V)
        out = out.transpose(0, 2, 1, 3).reshape(Bx, Tx, D)
        return out @ Wo.T + bo

    def _L0_ffn_ref(x, weight_fp8, bias, input_scale, weight_scale):
        import jax, jax.numpy as jnp
        import numpy as np
        FP8_MAX = 448.0
        x_q = jnp.clip(x / input_scale, -FP8_MAX, FP8_MAX)
        x_dq = x_q.astype(jnp.float8_e4m3fn).astype(x.dtype) * input_scale
        w_dq = weight_fp8 * weight_scale
        out = jnp.einsum('bsi,oi->bso', x_dq, w_dq) + bias
        return out
    h = _L0_tok_ref(x, L0_tok_tok_emb, L0_tok_pos_emb, L0_tok_W_in, L0_tok_conv_w, L0_tok_conv_b, L0_tok_W_B, L0_tok_W_C, L0_tok_D_vec, L0_tok_W_out, L0_tok_ln_g, L0_tok_ln_b)
    h = h + _L0_attn_ref(_layernorm(h, axis=-1), L0_attn_Wq, L0_attn_Wk, L0_attn_Wv, L0_attn_Wo, L0_attn_bo, L0_attn_planes_T, L0_attn_protos_T, L0_attn_logit_temp)
    h = h + _L0_ffn_ref(_layernorm(h, axis=-1), L0_ffn_weight_fp8, L0_ffn_bias, L0_ffn_input_scale, L0_ffn_weight_scale)
    return h

_drawn_inputs = setup_inputs


def setup_inputs(seed=0):
    import zlib

    import numpy as np

    out = dict(_drawn_inputs(seed))
    spreads = {'L0_tok_conv_b': (0.0, 0.8),
     'L0_tok_ln_g': (1.0, 0.2),
     'L0_tok_ln_b': (0.0, 0.1),
     'L0_attn_bo': (0.0, 0.1)}
    factors = {'L0_tok_W_in': 8.0,
     'L0_tok_conv_w': 8.0,
     'L0_tok_W_B': 8.0,
     'L0_tok_W_C': 8.0,
     'L0_tok_D_vec': 8.0,
     'L0_tok_W_out': 8.0,
     'L0_attn_planes_T': 3.639,
     'L0_attn_protos_T': 6.769}
    for name, (base, spread) in spreads.items():
        noise = np.random.default_rng([zlib.crc32(name.encode()), seed]).standard_normal(out[name].shape)
        drawn = base * np.exp(spread * noise) if base else spread * noise
        out[name] = jnp.asarray(drawn.astype(out[name].dtype))
    for name, factor in factors.items():
        out[name] = (out[name] * factor).astype(out[name].dtype)
    return out
```

```python
from contextlib import ExitStack

import concourse.bass as bass
from concourse import mybir

ALU = mybir.AluOpType
ACT = mybir.ActivationFunctionType
F32 = mybir.dt.float32
F32R = mybir.dt.float32r
I32 = mybir.dt.int32
U32 = mybir.dt.uint32
AX = mybir.AxisListType

P = 128
DECAY, INP = 0.95, 0.05
EPS = 1e-5
FP8_MAX = 448.0
PAR = 28


def after(step, k):
    return not isinstance(step, int) or step >= k


def tower_block(nc, t, x_res, ident, dims):
    SEQS, T, D, INNER, N, LAYERS = dims
    KC = D // P
    MC = INNER // P
    GT = 4 * T
    G = SEQS * T // GT
    TS = GT // P
    SLOTS = 8

    with ExitStack() as ctx:
        def sb(name, shape, dt=F32):
            return ctx.enter_context(nc.sbuf_tensor(name, shape, dt))

        def ps(name, shape, dt=F32):
            return ctx.enter_context(nc.psum_tensor(name, shape, dt))

        def sem(name):
            return ctx.enter_context(nc.semaphore(name))

        idx = sb("idx", [P, SEQS], I32)
        pos = sb("pos", [P, D])
        decay = sb("decay", [P, GT])
        half_neg = sb("half_neg", [P, TS])
        par_all = sb("par_all", [P, LAYERS, PAR])
        par = sb("par", [P, PAR])
        win_raw = sb("win_raw", [P, KC, 2 * INNER])
        wb_raw = sb("wb_raw", [P, MC, N])
        wc_raw = sb("wc_raw", [P, INNER])
        wo_raw = sb("wo_raw", [P, MC, D])
        win_h = sb("win_h", [P, KC, 2 * INNER], F32R)
        win_l = sb("win_l", [P, KC, 2 * INNER], F32R)
        wb_hl = sb("wb_hl", [P, MC, 2 * N], F32R)
        wc_h = sb("wc_h", [P, INNER], F32R)
        wc_l = sb("wc_l", [P, INNER], F32R)
        wo_h = sb("wo_h", [P, MC, D], F32R)
        wo_l = sb("wo_l", [P, MC, D], F32R)
        xh = [sb(f"xh{i}", [P, KC, GT], F32R) for i in range(2)]
        xl = [sb(f"xl{i}", [P, KC, GT], F32R) for i in range(2)]
        u = [[sb(f"u{i}{m}", [P, GT]) for m in range(MC)] for i in range(2)]
        gates_sb = sb("gates_sb", [P, 2, MC, GT])
        gate = [[gates_sb[:, i, m, :] for m in range(MC)] for i in range(2)]
        emb = gates_sb[:, 0].rearrange("p m (a d) -> p (m a) d", d=D)
        uh = sb("uh", [P, MC, GT], F32R)
        ul = sb("ul", [P, MC, GT], F32R)
        yh = sb("yh", [P, MC, GT], F32R)
        yl = sb("yl", [P, MC, GT], F32R)
        hs = sb("hs", [P, GT])
        hs_h = sb("hs_h", [P, GT], F32R)
        hs_l = sb("hs_l", [P, GT], F32R)
        zstat = sb("zstat", [P, TS, 6])
        zmv = sb("zmv", [P, TS, 2])
        zvar = sb("zvar", [P, TS])
        zrstd = sb("zrstd", [P, TS])
        zn = sb("zn", [P, TS, D])
        ident_r = sb("ident_r", [P, P], F32R)

        proj = [ps(f"proj{i}", [P, GT]) for i in range(4)]
        bu = ps("bu", [P, GT])
        z = [ps(f"z{i}", [P, 2, D]) for i in range(2)]
        zt = ps("zt", [P, GT])

        consts_loaded = sem("consts_loaded")
        consts_made = sem("consts_made")
        ident_zeroed = sem("ident_zeroed")
        gathered = [sem(f"gathered{j}") for j in range(SLOTS)]
        pos_added = sem("pos_added")
        emb_turned = sem("emb_turned")
        x_ready = sem("x_ready")
        raw_loaded = sem("raw_loaded")
        w_high = sem("w_high")
        w_split = sem("w_split")
        par_ready = sem("par_ready")
        x_high = sem("x_high")
        x_low = sem("x_low")
        in_proj = sem("in_proj")
        tap0 = sem("tap0")
        conv_tap = sem("conv_tap")
        gated = sem("gated")
        u_high = sem("u_high")
        u_full = sem("u_full")
        u_low = sem("u_low")
        bu_done = sem("bu_done")
        scanned = sem("scanned")
        hs_high = sem("hs_high")
        hs_low = sem("hs_low")
        hc_done = sem("hc_done")
        y_taken = sem("y_taken")
        y_full = sem("y_full")
        y_high = sem("y_high")
        y_low = sem("y_low")
        residual_in = sem("residual_in")
        z_done = sem("z_done")
        z_stat = sem("z_stat")
        z_mv = sem("z_mv")
        z_var = sem("z_var")
        z_rstd = sem("z_rstd")
        z_normed = sem("z_normed")
        z_turned = sem("z_turned")

        def pipeline(eng, body):
            for i in range(4):
                body(i, i % 2)
            with eng.Fori(2, G // 2 - 1) as pair:
                body(2 * pair, 0)
                body(2 * pair + 1, 1)
            for i in range(G - 2, G + 2):
                body(i, i % 2)

        def alive(g):
            return not isinstance(g, int) or 0 <= g < G

        with nc.Block() as block:

            @block.sync
            def _(sp):
                sp.dma_start(idx[:], t["tokens"]).then_inc(consts_loaded, 16)
                sp.dma_start(pos[:], t["pos_emb"][0:T, :]).then_inc(consts_loaded, 16)
                sp.dma_start(par_all[:], t["params"]).then_inc(consts_loaded, 16)
                def load_weights(layer):
                    for raw, name in ((win_raw, "win"), (wb_raw, "wb"), (wo_raw, "wo")):
                        sp.dma_start(raw[:], t[name][layer]).then_inc(raw_loaded, 16)
                    for half in range(2):
                        sp.dma_start(wc_raw[half * N:(half + 1) * N, :], t["wc"][layer]).then_inc(raw_loaded, 16)

                load_weights(0)
                with sp.Fori(1, LAYERS) as layer:
                    sp.wait_ge(w_split, 4 * layer)
                    load_weights(layer)

            @block.gpsimd
            def _(pool):
                nc.gpsimd.memset(half_neg[:], -0.5).then_inc(consts_made, 1)
                nc.gpsimd.memset(ident[:], 0.0).then_inc(ident_zeroed, 1)
                pool.wait_ge(ident_zeroed, 1)
                nc.gpsimd.affine_select(out=ident[:], in_=ident[:], compare_op=ALU.not_equal, fill=1.0, base=0,
                                        pattern=[[-1, P]], channel_multiplier=1).then_inc(consts_made, 1)
                pool.wait_ge(consts_loaded, 48)
                for n in range(SEQS):
                    if n >= SLOTS and n % 2 == 0:
                        pool.wait_ge(emb_turned, (n - SLOTS) // 2 + 1)
                    nc.gpsimd.indirect_dma_start(
                        emb[:, n % SLOTS, :], None, t["tok_emb"], bass.IndirectOffsetOnAxis(ap=idx[:, n:n + 1], axis=0),
                    ).then_inc(gathered[n % SLOTS], 16)

                def split_x(g, par_, s):
                    pool.wait_ge(x_high, s + 1)
                    nc.gpsimd.tensor_tensor(xl[par_][:], x_res[:, :, bass.ds(g * GT, GT)],
                                            xh[par_][:].bitcast(F32), ALU.subtract).then_inc(x_low, 1)

                def u_lows(g, q, s, ms):
                    for m in ms:
                        pool.wait_ge(u_full, 4 * s + m + 1)
                        if after(g, 1) and m == ms[0]:
                            pool.wait_ge(bu_done, s)
                        nc.gpsimd.tensor_tensor(ul[:, m, :], u[q][m][:], uh[:, m, :].bitcast(F32),
                                                ALU.subtract).then_inc(u_low, 1)

                with pool.Fori(0, LAYERS) as layer:
                    split_x(0, 0, layer * G)

                    def body(i, q):
                        s = layer * G + i
                        if alive(i):
                            u_lows(i, q, s, (0, 1))
                        if alive(i - 1):
                            for m in range(MC):
                                pool.wait_ge(y_high, 4 * (s - 1) + m + 1)
                                nc.gpsimd.tensor_tensor(yl[:, m, :], u[1 - q][m][:], yh[:, m, :].bitcast(F32),
                                                        ALU.subtract).then_inc(y_low, 1)
                        if alive(i):
                            u_lows(i, q, s, (2, 3))
                        if alive(i + 1):
                            split_x(i + 1, 1 - q, s + 1)
                        if alive(i - 1):
                            for t_ in range(TS // 2):
                                pool.wait_ge(z_var, 2 * (s - 1) + t_ + 1)
                                nc.gpsimd.tensor_tensor(zrstd[:, 2 * t_:2 * t_ + 2], zvar[:, 2 * t_:2 * t_ + 2],
                                                        half_neg[:, 0:2], ALU.pow).then_inc(z_rstd, 1)

                    pipeline(pool, body)

            @block.scalar
            def _(act):
                with act.Fori(0, SEQS // 4) as r:
                    for q in range(2):
                        act.wait_ge(emb_turned, 2 * r + q + 1)
                        nc.scalar.activation(x_res[:, :, bass.ds((2 * r + q) * 2 * T, 2 * T)],
                                             proj[q][:].rearrange("p (k t) -> p k t", k=KC),
                                             ACT.Copy).then_inc(x_ready, 1)

                with act.Fori(0, LAYERS) as layer:
                    act.wait_ge(raw_loaded, 80 * (layer + 1))
                    nc.scalar.activation(win_h[:], win_raw[:], ACT.Copy).then_inc(w_high, 1)
                    nc.scalar.activation(wb_hl[:, :, 0:N], wb_raw[:], ACT.Copy).then_inc(w_high, 1)
                    nc.scalar.activation(wc_h[:], wc_raw[:], ACT.Copy, scale=INP).then_inc(w_high, 1)
                    nc.scalar.activation(wo_h[:], wo_raw[:], ACT.Copy).then_inc(w_high, 1)
                    act.wait_ge(par_ready, layer + 1)

                    def body(i, q):
                        s = layer * G + i

                        def tap(m):
                            act.wait_ge(in_proj, 8 * s + 2 * m + 1)
                            nc.scalar.activation(u[q][m][:], proj[2 * (m % 2)][:], ACT.Identity,
                                                 bias=par[:, 16 + m:17 + m], scale=par[:, 4 * m + 3:4 * m + 4],
                                                 ).then_inc(tap0, 1)

                        def gates(m):
                            act.wait_ge(in_proj, 8 * s + 2 * m + 2)
                            nc.scalar.activation(gate[q][m], proj[2 * (m % 2) + 1][:], ACT.Silu).then_inc(gated, 1)

                        def silu(m):
                            act.wait_ge(conv_tap, 12 * s + 3 * m + 3)
                            if after(i, 1) and m == 0:
                                act.wait_ge(bu_done, s)
                            nc.scalar.activation(uh[:, m, :], u[q][m][:], ACT.Silu).then_inc(u_high, 1)
                            nc.scalar.activation(u[q][m][:], u[q][m][:], ACT.Silu).then_inc(u_full, 1)

                        if alive(i):
                            tap(0), gates(0), tap(1), gates(1), silu(0), silu(1)
                        if alive(i - 1):
                            for m in range(MC):
                                act.wait_ge(y_full, 4 * (s - 1) + m + 1)
                                nc.scalar.activation(yh[:, m, :], u[1 - q][m][:], ACT.Copy).then_inc(y_high, 1)
                        if alive(i):
                            tap(2), gates(2), tap(3), gates(3), silu(2), silu(3)
                        if alive(i - 2):
                            for k in range(KC):
                                act.wait_ge(z_turned, 2 * (s - 2) + k + 1)
                                nc.scalar.activation(x_res[:, k, bass.ds((i - 2) * GT, GT)], zt[:], ACT.Identity,
                                                     bias=par[:, 26 + k:27 + k], scale=par[:, 24 + k:25 + k],
                                                     ).then_inc(x_ready, 1)

                    pipeline(act, body)

            @block.vector
            def _(dve):
                nc.vector.memset(decay[:], DECAY).then_inc(consts_made, 1)
                dve.wait_ge(consts_made, 3)
                nc.vector.memset(decay[:].rearrange("p (s t) -> p s t", t=T)[:, :, 0:1], 0.0).then_inc(consts_made, 1)
                nc.vector.tensor_copy(ident_r[:], ident[:]).then_inc(consts_made, 1)
                dve.wait_ge(consts_loaded, 48)
                dve.wait_ge(consts_made, 5)
                with dve.Fori(0, SEQS // SLOTS) as r:
                    for j in range(SLOTS):
                        dve.wait_ge(gathered[j], 16 * r + 16)
                        nc.vector.tensor_tensor(emb[:, j, :], emb[:, j, :], pos[:], ALU.add).then_inc(pos_added, 1)

                def split_x(g, q, s):
                    dve.wait_ge(x_ready, 2 * s + 2)
                    nc.vector.tensor_copy(xh[q][:], x_res[:, :, bass.ds(g * GT, GT)]).then_inc(x_high, 1)

                with dve.Fori(0, LAYERS) as layer:
                    dve.wait_ge(x_ready, 2 * G * (layer + 1))
                    nc.vector.tensor_copy(par[:], par_all[:, bass.ds(layer, 1), :]).then_inc(par_ready, 1)
                    split_x(0, 0, layer * G)
                    dve.wait_ge(w_high, 4 * layer + 1)
                    nc.vector.tensor_tensor(win_l[:], win_raw[:], win_h[:].bitcast(F32), ALU.subtract).then_inc(w_split, 1)
                    dve.wait_ge(w_high, 4 * layer + 4)
                    nc.vector.tensor_tensor(wb_hl[:, :, N:2 * N], wb_raw[:], wb_hl[:, :, 0:N].bitcast(F32),
                                            ALU.subtract).then_inc(w_split, 1)
                    nc.vector.scalar_tensor_tensor(wc_l[:], wc_raw[:], INP, wc_h[:].bitcast(F32), ALU.mult,
                                                   ALU.subtract).then_inc(w_split, 1)
                    nc.vector.tensor_tensor(wo_l[:], wo_raw[:], wo_h[:].bitcast(F32), ALU.subtract).then_inc(w_split, 1)
                    dve.wait_ge(par_ready, layer + 1)

                    def body(i, q):
                        s = layer * G + i

                        def conv(m):
                            dve.wait_ge(tap0, 4 * s + m + 1)
                            src = proj[2 * (m % 2)][:].rearrange("p (s t) -> p s t", t=T)
                            dst = u[q][m][:].rearrange("p (s t) -> p s t", t=T)
                            for n in range(1, 4):
                                if n > 1:
                                    dve.wait_ge(conv_tap, 12 * s + 3 * m + n - 1)
                                nc.vector.scalar_tensor_tensor(
                                    dst[:, :, n:T], src[:, :, 0:T - n], par[:, 4 * m + 3 - n:4 * m + 4 - n],
                                    dst[:, :, n:T], ALU.mult, ALU.add).then_inc(conv_tap, 1)

                        if alive(i):
                            conv(0), conv(1)
                        if alive(i - 1):
                            for m in range(MC):
                                dve.wait_ge(hc_done, 4 * (s - 1) + m + 1)
                                nc.vector.scalar_tensor_tensor(u[1 - q][m][:], u[1 - q][m][:], par[:, 20 + m:21 + m],
                                                               proj[m][:], ALU.mult, ALU.add).then_inc(y_taken, 1)
                                dve.wait_ge(y_taken, 4 * (s - 1) + m + 1)
                                nc.vector.tensor_tensor(u[1 - q][m][:], u[1 - q][m][:], gate[1 - q][m], ALU.mult
                                                        ).then_inc(y_full, 1)
                        if alive(i):
                            conv(2), conv(3)
                        if alive(i + 1):
                            if alive(i - 1):
                                dve.wait_ge(residual_in, s)
                            split_x(i + 1, 1 - q, s + 1)
                        if alive(i - 1):
                            for k in range(TS):
                                dve.wait_ge(z_done, 2 * (s - 1) + k // 2 + 1)
                                nc.vector.bn_stats(zstat[:, k, :], z[k // 2][:, k % 2, :]).then_inc(z_stat, 1)
                                dve.wait_ge(consts_made, 5)
                                dve.wait_ge(z_stat, 4 * (s - 1) + k + 1)
                                nc.vector.bn_aggr(zmv[:, k, :], zstat[:, k, :]).then_inc(z_mv, 1)
                                if k % 2:
                                    dve.wait_ge(z_mv, 4 * (s - 1) + k + 1)
                                    nc.vector.tensor_scalar(zvar[:, k - 1:k + 1], zmv[:, k - 1:k + 1, 1], EPS, None,
                                                            ALU.add).then_inc(z_var, 1)
                        if alive(i):
                            dve.wait_ge(bu_done, s + 1)
                            nc.vector.tensor_tensor_scan(hs[:], decay[:], bu[:], 0.0, ALU.mult, ALU.add
                                                         ).then_inc(scanned, 1)
                            dve.wait_ge(scanned, s + 1)
                            nc.vector.tensor_copy(hs_h[:], hs[:]).then_inc(hs_high, 1)
                            dve.wait_ge(hs_high, s + 1)
                            nc.vector.tensor_tensor(hs_l[:], hs[:], hs_h[:].bitcast(F32), ALU.subtract
                                                    ).then_inc(hs_low, 1)
                        if alive(i - 1):
                            if after(i - 1, 1):
                                dve.wait_ge(z_turned, 2 * (s - 1))
                            for k in range(TS):
                                dve.wait_ge(z_rstd, 2 * (s - 1) + k // 2 + 1)
                                nc.vector.tensor_scalar(zn[:, k, :], z[k // 2][:, k % 2, :], zmv[:, k, 0:1],
                                                        zrstd[:, k:k + 1], ALU.subtract, ALU.mult
                                                        ).then_inc(z_normed, 1)

                    pipeline(dve, body)

            @block.tensor
            def _(pe):
                pe.wait_ge(consts_made, 5)
                def turn_rows(r):
                    for j in range(SLOTS):
                        pair = j // 2
                        pe.wait_ge(pos_added, r * SLOTS + j + 1)
                        if j % 2 == 0 and (after(r, 1) or pair >= 2):
                            pe.wait_ge(x_ready, (SLOTS // 2) * r + pair - 1)
                        for k in range(KC):
                            last = nc.tensor.transpose(
                                proj[pair % 2][:, k * 2 * T + (j % 2) * T:k * 2 * T + (j % 2) * T + T],
                                emb[:, j, k * P:(k + 1) * P], ident[:])
                        if j % 2:
                            last.then_inc(emb_turned, 1)

                turn_rows(0)
                with pe.Fori(1, SEQS // SLOTS) as r:
                    turn_rows(r)

                with pe.Fori(0, LAYERS) as layer:
                    def body(i, q):
                        s = layer * G + i

                        def in_unit(m, is_gate):
                            bank = proj[2 * (m % 2) + is_gate]
                            if m < 2:
                                if after(i, 1):
                                    if is_gate:
                                        pe.wait_ge(gated, 4 * (s - 1) + m + 3)
                                    else:
                                        pe.wait_ge(conv_tap, 12 * (s - 1) + 3 * (m + 2) + 3)
                            elif after(i, 1):
                                pe.wait_ge(y_taken, 4 * (s - 1) + 2 * (m - 2) + is_gate + 1)
                            elif is_gate:
                                pe.wait_ge(gated, 4 * s + m - 1)
                            else:
                                pe.wait_ge(conv_tap, 12 * s + 3 * (m - 2) + 3)
                            c = is_gate * INNER + m * P
                            n = 0
                            for w, x in ((win_h, xh), (win_h, xl), (win_l, xh)):
                                for k in range(KC):
                                    last = nc.tensor.matmul(bank[:], w[:, k, c:c + P], x[q][:, k, :],
                                                            start=(n == 0), stop=(n == 5))
                                    n += 1
                            last.then_inc(in_proj, 1)

                        if alive(i):
                            pe.wait_ge(w_split, 4 * layer + 4)
                            pe.wait_ge(x_low, s + 1)
                            for m in range(2):
                                in_unit(m, 0), in_unit(m, 1)
                        if alive(i - 1):
                            pe.wait_ge(hs_low, s)
                            for m in range(MC):
                                if alive(i):
                                    if m % 2:
                                        pe.wait_ge(gated, 4 * s + m // 2 + 1)
                                    else:
                                        pe.wait_ge(conv_tap, 12 * s + 3 * (m // 2) + 3)
                                for n, (w, h) in enumerate(((wc_h, hs_h), (wc_h, hs_l), (wc_l, hs_h))):
                                    last = nc.tensor.matmul(proj[m][:], w[:, m * P:(m + 1) * P], h[:],
                                                            start=(n == 0), stop=(n == 2))
                                last.then_inc(hc_done, 1)
                        if alive(i):
                            for m in range(2, MC):
                                in_unit(m, 0), in_unit(m, 1)
                        if alive(i - 2):
                            for k in range(KC):
                                pe.wait_ge(z_normed, 4 * (s - 1))
                                if k:
                                    pe.wait_ge(x_ready, 2 * G + 2 * (s - 2) + k)
                                elif after(i - 2, 1):
                                    pe.wait_ge(x_ready, 2 * G + 2 * (s - 2))
                                for j in range(TS):
                                    last = nc.tensor.transpose(zt[:, j * P:(j + 1) * P],
                                                               zn[:, j, k * P:(k + 1) * P], ident[:])
                                last.then_inc(z_turned, 1)
                        if alive(i - 1):
                            if after(i - 1, 1):
                                pe.wait_ge(z_normed, 4 * (s - 1))
                            for j in range(TS):
                                for k in range(KC):
                                    for n, x in enumerate((xh, xl)):
                                        last = nc.tensor.matmul(
                                            z[j // 2][:, j % 2, k * P:(k + 1) * P], x[1 - q][:, k, j * P:(j + 1) * P],
                                            ident_r[:], start=(j % 2 == 0 and k == 0 and n == 0), stop=False,
                                            skip_group_check=True)
                            last.then_inc(residual_in, 1)
                            pe.wait_ge(y_low, 4 * s)
                            for j in range(TS):
                                for m in range(MC):
                                    for n, (a, w) in enumerate(((yh, wo_h), (yh, wo_l), (yl, wo_h))):
                                        last = nc.tensor.matmul(
                                            z[j // 2][:, j % 2, :], a[:, m, j * P:(j + 1) * P], w[:, m, :],
                                            start=False, stop=(m == MC - 1 and n == 2), skip_group_check=True)
                                if j % 2:
                                    last.then_inc(z_done, 1)
                        if alive(i):
                            if after(i, 1):
                                pe.wait_ge(scanned, s)
                            for m in range(MC):
                                pe.wait_ge(u_low, 4 * s + m + 1)
                                nc.tensor.matmul(bu[:], wb_hl[:, m, :], uh[:, m, :], start=(m == 0), stop=False)
                                last = nc.tensor.matmul(bu[:], wb_hl[:, m, :], ul[:, m, :], start=False,
                                                        stop=(m == MC - 1))
                            last.then_inc(bu_done, 1)

                    pipeline(pe, body)


def attention_block(nc, t, x_res, ident, out, dims):
    SEQS, T, D, HEADS, TABLES, BITS = dims
    HD = D // HEADS
    R = 1 << BITS
    S = TABLES * R
    KC = D // P
    HC = 4
    HQ = HEADS // HC
    W = P // HQ

    with ExitStack() as ctx:
        def sb(name, shape, dt=F32):
            return ctx.enter_context(nc.sbuf_tensor(name, shape, dt))

        def two(name, shape, dt=F32):
            return [sb(f"{name}{i}", shape, dt) for i in range(2)]

        def ps(name, shape, dt=F32):
            return ctx.enter_context(nc.psum_tensor(name, shape, dt))

        def sem(name):
            return ctx.enter_context(nc.semaphore(name))

        pe_t = two("pe_t", [P, HQ, HC, T])
        raw, wkv_raw = (tile[:, 0:2].rearrange("p (k a) c t -> p k (a c t)", k=KC) for tile in pe_t)
        wq_h, wq_l = sb("wq_h", [P, KC, HEADS * W], F32R), sb("wq_l", [P, KC, HEADS * W], F32R)
        wkv_h, wkv_l = sb("wkv_h", [P, KC, HEADS * W], F32R), sb("wkv_l", [P, KC, HEADS * W], F32R)
        wk_rows = sb("wk_rows", [P, KC, D])
        planes = sb("planes", [P, P // HD * W])
        wp_h, wp_l = sb("wp_h", [P, KC, HEADS * W], F32R), sb("wp_l", [P, KC, HEADS * W], F32R)
        protos = sb("protos", [P, HQ * S])
        wo_raw = sb("awo_raw", [P, KC, D])
        wo_h, wo_l = sb("awo_h", [P, KC, D], F32R), sb("awo_l", [P, KC, D], F32R)
        wf_raw = sb("wf_raw", [P, KC, D])
        wf_h, wf_l = sb("wf_h", [P, KC, D], F32R), sb("wf_l", [P, KC, D], F32R)
        bo = sb("bo", [P, D])
        bias = sb("bias", [P, D])
        scal = sb("scal", [P, 8])
        half_neg = sb("ahalf_neg", [P, 1])
        xs = two("xs", [P, KC, T])
        xt = two("xt", [P, D])
        stat, mv, var, rstd = sb("stat", [P, 6]), sb("mv", [P, 2]), sb("var", [P, 1]), sb("rstd", [P, 1])
        nt = two("nt", [P, D])
        nh, nl = two("nh", [P, KC, T], F32R), two("nl", [P, KC, T], F32R)
        qp = two("qp", [P, HC, T])
        kv = two("kv", [P, HEADS * W])
        th = two("th", [P, HC, T])
        lmax = sb("lmax", [P, HC, HQ * TABLES])
        e = two("e", [P, HC, HQ * S])
        lsum = sb("lsum", [P, HC, HQ * TABLES])
        lrec = two("lrec", [P, HC, HQ * TABLES])
        bk = two("bk", [P, HEADS, W])
        bv = two("bv", [P, HEADS, HD + 1])
        bkt = two("bkt", [P, HC, S])
        mp = two("mp", [P, HC, HQ, W])
        qa = two("qa", [P, HC, T])
        osum = sb("osum", [P, HEADS])
        ot = two("ot", [P, D])
        oh, ol = two("oh", [P, KC, T], F32R), two("ol", [P, KC, T], F32R)
        h = two("h", [P, D])
        hb = two("hb", [P, D])
        stat2, mv2, var2, rstd2 = sb("stat2", [P, 6]), sb("mv2", [P, 2]), sb("var2", [P, 1]), sb("rstd2", [P, 1])
        v = sb("v", [P, D])
        ulp = sb("ulp", [P, D])
        qv = two("qv", [P, D])
        qt = two("qt", [P, KC, T], F32R)
        res = two("res", [P, D])

        big = [ps(f"big{i}", [P, 512]) for i in range(4)]
        m0, m1, m2, m3 = (ps(f"misc{i}", [P, 512]) for i in range(4))

        names = """loaded zeroed made scales blocks raw_high w_done wp_in
            xs_copied x_turned stat_in mv_in var_in rstd_in xt_in n_in n_turned n_high n_low
            q_done kv_done proj_done qp_in kv_in th_in logits_in lmax_in shifted e_in lsum_in lrec_in p_in
            bucket_in bk_in bv_in bk_turned bkt_in s_in smax_in m_turned qa_in st_in et_in pv_in osum_in ot_in
            o_turned o_high o_low y_in h_in hb_in stat2_in mv2_in var2_in rstd2_in quant qv_in q_turned qt_in
            f_in res_in""".split()
        sg = {n: sem("a_" + n) for n in names}
        out_sent = [sem(f"out_sent{i}") for i in range(2)]

        def alive(b):
            return not isinstance(b, int) or 0 <= b < SEQS

        def pipeline(eng, body):
            for i in range(4):
                body(i, i % 2)
            with eng.Fori(2, SEQS // 2 - 1) as pair:
                body(2 * pair, 0)
                body(2 * pair + 1, 1)
            for i in range(SEQS - 2, SEQS + 2):
                body(i, i % 2)

        with nc.Block() as block:

            @block.sync
            def _(sp):
                sp.dma_start(raw[:], t["wq"]).then_inc(sg["loaded"], 16)
                sp.dma_start(wkv_raw[:], t["wkv"]).then_inc(sg["loaded"], 16)
                sp.dma_start(wk_rows[:], t["wk_rows"]).then_inc(sg["loaded"], 16)
                sp.dma_start(wo_raw[:], t["wo_attn"]).then_inc(sg["loaded"], 16)
                sp.dma_start(wf_raw[:], t["wf"]).then_inc(sg["loaded"], 16)
                for tile, name in ((bo, "bo"), (bias, "bias")):
                    sp.dma_start(tile[:], t[name].partition_broadcast(P)).then_inc(sg["loaded"], 16)
                for c, name in enumerate(("logit_temp", "input_scale", "weight_scale")):
                    sp.dma_start(scal[:, c:c + 1], t[name].partition_broadcast(P)).then_inc(sg["loaded"], 16)
                sp.wait_ge(sg["zeroed"], 2)
                for j in range(P // HD):
                    sp.dma_start(planes[j * HD:(j + 1) * HD, j * W:(j + 1) * W], t["planes"]).then_inc(sg["blocks"], 16)
                for j in range(HQ * TABLES):
                    sp.dma_start(protos[j * BITS:(j + 1) * BITS, j * R:(j + 1) * R], t["protos"]
                                 ).then_inc(sg["blocks"], 16)
                def body(i, q):
                    b = i - 2
                    if alive(b):
                        sp.wait_ge(sg["res_in"], b + 1)
                        sp.dma_start(out[bass.ds(b, 1), :, :].rearrange("b t d -> t (b d)"), res[q][:]
                                     ).then_inc(out_sent[q], 16)
                pipeline(sp, body)
                for q in range(2):
                    sp.wait_ge(out_sent[q], 16 * (SEQS // 2))

            @block.gpsimd
            def _(pool):
                nc.gpsimd.memset(planes[:], 0.0).then_inc(sg["zeroed"], 1)
                nc.gpsimd.memset(protos[:], 0.0).then_inc(sg["zeroed"], 1)
                nc.gpsimd.memset(half_neg[:], -0.5).then_inc(sg["made"], 1)
                for q in range(2):
                    nc.gpsimd.memset(bk[q][:, :, HD:W], 0.0).then_inc(sg["made"], 1)
                    nc.gpsimd.memset(bv[q][:, :, HD:HD + 1], 1.0).then_inc(sg["made"], 1)
                    nc.gpsimd.memset(mp[q][:], 0.0).then_inc(sg["made"], 1)
                pool.wait_ge(sg["made"], 7)
                for q in range(2):
                    nc.gpsimd.memset(bk[q][:, :, HD:HD + 1], 1.0).then_inc(sg["made"], 1)

                def copy_x(b, q):
                    if after(b, 2):
                        pool.wait_ge(sg["x_turned"], b - 1)
                    nc.gpsimd.tensor_copy(xs[q][:], x_res[:, :, bass.ds(b * T, T)]).then_inc(sg["xs_copied"], 1)

                copy_x(0, 0)

                def body(i, q):
                    if alive(i):
                        pool.wait_ge(sg["var_in"], i + 1)
                        nc.gpsimd.tensor_tensor(rstd[:], var[:], half_neg[:], ALU.pow).then_inc(sg["rstd_in"], 1)
                    if alive(i - 2):
                        b = i - 2
                        pool.wait_ge(sg["var2_in"], b + 1)
                        nc.gpsimd.tensor_tensor(rstd2[:], var2[:], half_neg[:], ALU.pow).then_inc(sg["rstd2_in"], 1)
                        if after(b, 2):
                            pool.wait_ge(sg["res_in"], b - 1)
                        nc.gpsimd.tensor_tensor(hb[q][:], h[q][:], bias[:], ALU.add).then_inc(sg["hb_in"], 1)
                    if alive(i + 1):
                        copy_x(i + 1, 1 - q)
                    if alive(i):
                        for c in range(HC):
                            pool.wait_ge(sg["lrec_in"], 4 * i + c + 1)
                            ev = e[q][:, c, :].rearrange("p (a r) -> p a r", r=R)
                            rv = lrec[q][:, c, :].unsqueeze(2).broadcast_to([P, HQ * TABLES, R])
                            nc.gpsimd.tensor_tensor(ev, ev, rv, ALU.mult).then_inc(sg["p_in"], 1)

                pipeline(pool, body)

            @block.scalar
            def _(act):
                act.wait_ge(sg["loaded"], 160)
                nc.scalar.activation(scal[:, 3:4], scal[:, 0:1], ACT.Exp).then_inc(sg["raw_high"], 1)
                nc.scalar.activation(wq_h[:], raw[:], ACT.Identity, scale=HD ** -0.5).then_inc(sg["raw_high"], 1)
                nc.scalar.activation(wkv_h[:], wkv_raw[:], ACT.Copy).then_inc(sg["raw_high"], 1)
                nc.scalar.activation(wo_h[:], wo_raw[:], ACT.Copy).then_inc(sg["raw_high"], 1)
                act.wait_ge(sg["w_done"], 1)
                nc.scalar.activation(wf_h[:], wf_raw[:], ACT.Copy).then_inc(sg["raw_high"], 1)
                for k in range(KC):
                    act.wait_ge(sg["wp_in"], k + 1)
                    nc.scalar.activation(wp_h[:, k, :], big[k][:], ACT.Copy).then_inc(sg["raw_high"], 1)

                def body(i, q):
                    if alive(i - 2):
                        b = i - 2
                        act.wait_ge(sg["o_turned"], b + 1)
                        nc.scalar.activation(oh[q][:], m2[:, 0:D].rearrange("p (k t) -> p k t", k=KC), ACT.Copy
                                             ).then_inc(sg["o_high"], 1)
                    if alive(i - 1):
                        b, r = i - 1, 1 - q
                        act.wait_ge(sg["bucket_in"], b + 1)
                        nc.scalar.activation(bk[r][:, :, 0:HD], m1[:].rearrange("p (h w) -> p h w", w=W)[:, :, 0:HD],
                                             ACT.Copy).then_inc(sg["bk_in"], 1)
                        act.wait_ge(sg["bk_turned"], b + 1)
                        nc.scalar.activation(bkt[r][:], m3[:].rearrange("p (c s) -> p c s", c=HC), ACT.Copy
                                             ).then_inc(sg["bkt_in"], 1)
                    if alive(i):
                        act.wait_ge(sg["n_turned"], i + 1)
                        nc.scalar.activation(nh[q][:], m0[:, D:2 * D].rearrange("p (k t) -> p k t", k=KC), ACT.Copy
                                             ).then_inc(sg["n_high"], 1)
                        act.wait_ge(sg["q_done"], i + 1)
                        nc.scalar.activation(qp[q][:], m1[:].rearrange("p (c t) -> p c t", c=HC), ACT.Copy
                                             ).then_inc(sg["qp_in"], 1)
                        act.wait_ge(sg["proj_done"], i + 1)
                        nc.scalar.activation(th[q][:], m0[:].rearrange("p (c t) -> p c t", c=HC), ACT.Tanh
                                             ).then_inc(sg["th_in"], 1)

                    def exp_logits(c):
                        act.wait_ge(sg["shifted"], 4 * i + c + 1)
                        nc.scalar.activation(e[q][:, c, :], e[q][:, c, :], ACT.Exp).then_inc(sg["e_in"], 1)

                    def exp_scores(j):
                        b, r = i - 1, 1 - q
                        act.wait_ge(sg["st_in"], 4 * b + j + 1)
                        nc.scalar.activation(pe_t[r][:, j, :, :], big[2 + j % 2][:].rearrange(
                            "p (c t) -> p c t", c=HC), ACT.Exp).then_inc(sg["et_in"], 1)

                    for c in range(2):
                        if alive(i):
                            exp_logits(c)
                    for j in range(2):
                        if alive(i - 1):
                            exp_scores(j)
                    for c in range(2, 4):
                        if alive(i):
                            exp_logits(c)
                    for j in range(2, 4):
                        if alive(i - 1):
                            exp_scores(j)
                    if alive(i - 2):
                        b = i - 2
                        act.wait_ge(sg["q_turned"], b + 1)
                        nc.scalar.activation(qt[q][:], m2[:, 0:D].rearrange("p (k t) -> p k t", k=KC), ACT.Copy
                                             ).then_inc(sg["qt_in"], 1)

                pipeline(act, body)

            @block.vector
            def _(dve):
                dve.wait_ge(sg["raw_high"], 1)
                nc.vector.tensor_scalar(scal[:, 3:4], scal[:, 3:4], 0.01, 20.0, ALU.max, ALU.min).then_inc(sg["scales"], 1)
                nc.vector.tensor_tensor(scal[:, 5:6], scal[:, 1:2], scal[:, 2:3], ALU.mult).then_inc(sg["scales"], 1)
                nc.vector.reciprocal(scal[:, 6:7], scal[:, 1:2]).then_inc(sg["scales"], 1)
                dve.wait_ge(sg["scales"], 3)
                nc.vector.reciprocal(scal[:, 4:5], scal[:, 3:4]).then_inc(sg["scales"], 1)
                nc.vector.tensor_scalar(wf_raw[:], wf_raw[:], scal[:, 5:6], None, ALU.mult).then_inc(sg["w_done"], 1)
                dve.wait_ge(sg["scales"], 4)
                dve.wait_ge(sg["blocks"], 16 * (P // HD + HQ * TABLES))
                nc.vector.tensor_scalar(protos[:], protos[:], scal[:, 4:5], None, ALU.mult).then_inc(sg["w_done"], 1)
                dve.wait_ge(sg["raw_high"], 7)
                dve.wait_ge(sg["w_done"], 2)
                nc.vector.scalar_tensor_tensor(wq_l[:], raw[:], HD ** -0.5, wq_h[:].bitcast(F32), ALU.mult, ALU.subtract
                                               ).then_inc(sg["w_done"], 1)
                for lo, full, hi in ((wkv_l, wkv_raw, wkv_h), (wo_l, wo_raw, wo_h), (wf_l, wf_raw, wf_h)):
                    nc.vector.tensor_tensor(lo[:], full[:], hi[:].bitcast(F32), ALU.subtract).then_inc(sg["w_done"], 1)
                for k in range(KC):
                    nc.vector.tensor_tensor(wp_l[:, k, :], big[k][:], wp_h[:, k, :].bitcast(F32), ALU.subtract
                                            ).then_inc(sg["w_done"], 1)

                def front(i, q):
                    dve.wait_ge(sg["x_turned"], i + 1)
                    nc.vector.bn_stats(stat[:], m0[:, 0:D]).then_inc(sg["stat_in"], 1)
                    dve.wait_ge(sg["made"], 9)
                    dve.wait_ge(sg["stat_in"], i + 1)
                    nc.vector.bn_aggr(mv[:], stat[:]).then_inc(sg["mv_in"], 1)
                    dve.wait_ge(sg["mv_in"], i + 1)
                    nc.vector.tensor_scalar(var[:], mv[:, 1:2], EPS, None, ALU.add).then_inc(sg["var_in"], 1)

                def front_norm(i, q):
                    dve.wait_ge(sg["rstd_in"], i + 1)
                    nc.vector.tensor_scalar(nt[q][:], m0[:, 0:D], mv[:, 0:1], rstd[:, 0:1], ALU.subtract, ALU.mult
                                            ).then_inc(sg["n_in"], 1)

                def body(i, q):
                    if alive(i):
                        front(i, q)
                    if alive(i - 1):
                        b, r = i - 1, 1 - q
                        dve.wait_ge(sg["bucket_in"], b + 1)
                        dve.wait_ge(sg["bk_in"], b + 1)
                        nc.vector.tensor_copy(bv[r][:, :, 0:HD], m1[:].rearrange("p (h w) -> p h w", w=W)[:, :, HD:W]
                                              ).then_inc(sg["bv_in"], 1)
                    if alive(i):
                        front_norm(i, q)
                    if alive(i - 2):
                        b = i - 2
                        dve.wait_ge(sg["o_high"], b + 1)
                        nc.vector.tensor_tensor(ol[q][:], m2[:, 0:D].rearrange("p (k t) -> p k t", k=KC),
                                                oh[q][:].bitcast(F32), ALU.subtract).then_inc(sg["o_low"], 1)
                        dve.wait_ge(sg["y_in"], b + 1)
                        if after(b, 2):
                            dve.wait_ge(sg["hb_in"], b - 1)
                        nc.vector.tensor_tensor(h[q][:], m2[:, D:2 * D], xt[q][:], ALU.add).then_inc(sg["h_in"], 1)
                        dve.wait_ge(sg["h_in"], b + 1)
                        nc.vector.bn_stats(stat2[:], h[q][:]).then_inc(sg["stat2_in"], 1)
                        dve.wait_ge(sg["made"], 9)
                        dve.wait_ge(sg["stat2_in"], b + 1)
                        nc.vector.bn_aggr(mv2[:], stat2[:]).then_inc(sg["mv2_in"], 1)
                        dve.wait_ge(sg["mv2_in"], b + 1)
                        nc.vector.tensor_scalar(var2[:], mv2[:, 1:2], EPS, None, ALU.add).then_inc(sg["var2_in"], 1)
                    if alive(i):
                        dve.wait_ge(sg["n_high"], i + 1)
                        nc.vector.tensor_tensor(xt[q][:], m0[:, 0:D], bo[:], ALU.add).then_inc(sg["xt_in"], 1)
                        nc.vector.tensor_tensor(nl[q][:], m0[:, D:2 * D].rearrange("p (k t) -> p k t", k=KC),
                                                nh[q][:].bitcast(F32), ALU.subtract).then_inc(sg["n_low"], 1)
                    if alive(i - 1):
                        b, r = i - 1, 1 - q
                        for j in range(HQ):
                            dve.wait_ge(sg["s_in"], 4 * b + j + 1)
                            nc.vector.tensor_reduce(mp[r][:, :, j, HD], big[j][:].rearrange("p (c s) -> p c s", c=HC),
                                                    AX.X, ALU.max, negate=True).then_inc(sg["smax_in"], 1)
                    if alive(i):
                        dve.wait_ge(sg["kv_done"], i + 1)
                        nc.vector.tensor_copy(kv[q][:], m3[:]).then_inc(sg["kv_in"], 1)

                    def shift(c):
                        bank = big[[0, 1, 0, 1][c]][:].rearrange("p (a r) -> p a r", r=R)
                        dve.wait_ge(sg["logits_in"], 4 * i + c + 1)
                        nc.vector.tensor_reduce(lmax[:, c, :], bank, AX.X, ALU.max).then_inc(sg["lmax_in"], 1)
                        dve.wait_ge(sg["lmax_in"], 4 * i + c + 1)
                        nc.vector.tensor_tensor(e[q][:, c, :].rearrange("p (a r) -> p a r", r=R), bank,
                                                lmax[:, c, :].unsqueeze(2).broadcast_to([P, HQ * TABLES, R]),
                                                ALU.subtract).then_inc(sg["shifted"], 1)

                    def total(c):
                        dve.wait_ge(sg["e_in"], 4 * i + c + 1)
                        nc.vector.tensor_reduce(lsum[:, c, :], e[q][:, c, :].rearrange("p (a r) -> p a r", r=R),
                                                AX.X, ALU.add).then_inc(sg["lsum_in"], 1)
                        dve.wait_ge(sg["lsum_in"], 4 * i + c + 1)
                        nc.vector.reciprocal(lrec[q][:, c, :], lsum[:, c, :]).then_inc(sg["lrec_in"], 1)

                    if alive(i - 1):
                        b, r = i - 1, 1 - q
                        dve.wait_ge(sg["m_turned"], b + 1)
                        nc.vector.tensor_tensor(qa[r][:], m3[:].rearrange("p (c t) -> p c t", c=HC), qp[r][:], ALU.add
                                                ).then_inc(sg["qa_in"], 1)
                    if alive(i):
                        shift(0), shift(1), total(0)
                    if alive(i - 2):
                        b = i - 2
                        step = [0]

                        def chain(ins):
                            step[0] += 1
                            ins.then_inc(sg["quant"], 1)
                            dve.wait_ge(sg["quant"], 7 * b + step[0])

                        dve.wait_ge(sg["rstd2_in"], b + 1)
                        chain(nc.vector.tensor_scalar(v[:], h[q][:], mv2[:, 0:1], rstd2[:, 0:1], ALU.subtract, ALU.mult))
                        chain(nc.vector.tensor_scalar(v[:], v[:], scal[:, 6:7], FP8_MAX, ALU.mult, ALU.min))
                        chain(nc.vector.tensor_scalar(v[:], v[:], -FP8_MAX, None, ALU.max))
                        chain(nc.vector.tensor_scalar(ulp[:].bitcast(U32), v[:].bitcast(U32), 0x7F800000, None,
                                                      ALU.bitwise_and))
                        chain(nc.vector.tensor_scalar(ulp[:], ulp[:], 2.0 ** -6, 1.5 * 2.0 ** 20, ALU.max, ALU.mult))
                        chain(nc.vector.tensor_tensor(v[:], v[:], ulp[:], ALU.add))
                        if after(b, 2):
                            dve.wait_ge(sg["q_turned"], b - 1)
                        chain(nc.vector.tensor_tensor(qv[q][:], v[:], ulp[:], ALU.subtract))
                    if alive(i):
                        shift(2), shift(3), total(1), total(2), total(3)
                    if alive(i - 2):
                        b = i - 2
                        dve.wait_ge(sg["f_in"], b + 1)
                        dve.wait_ge(sg["hb_in"], b + 1)
                        if after(b, 2):
                            dve.wait_ge(out_sent[q], 8 * (b - q))
                        nc.vector.tensor_tensor(res[q][:], m2[:, D:2 * D], hb[q][:], ALU.add).then_inc(sg["res_in"], 1)
                    if alive(i - 1):
                        b, r = i - 1, 1 - q
                        dve.wait_ge(sg["pv_in"], b + 1)
                        ov = m1[:, 0:HEADS * (HD + 1)].rearrange("p (h w) -> p h w", w=HD + 1)
                        nc.vector.reciprocal(osum[:], ov[:, :, HD]).then_inc(sg["osum_in"], 1)
                        dve.wait_ge(sg["osum_in"], b + 1)
                        nc.vector.tensor_tensor(ot[r][:].rearrange("p (h w) -> p h w", w=HD), ov[:, :, 0:HD],
                                                osum[:].unsqueeze(2).broadcast_to([P, HEADS, HD]), ALU.mult
                                                ).then_inc(sg["ot_in"], 1)

                pipeline(dve, body)

            @block.tensor
            def _(pe):
                pe.wait_ge(sg["loaded"], 160)
                pe.wait_ge(sg["blocks"], 16 * (P // HD + HQ * TABLES))
                for k in range(KC):
                    for c in range(KC):
                        last = nc.tensor.matmul(big[k][:, c * 256:(c + 1) * 256], wk_rows[:, c, k * P:(k + 1) * P],
                                                planes[:], start=True, stop=True)
                    last.then_inc(sg["wp_in"], 1)
                pe.wait_ge(sg["w_done"], 8)
                pe.wait_ge(sg["made"], 9)

                def three(outp, a, b, lhs_high, lhs_low, rhs_high, rhs_low, kc):
                    n = 0
                    for l, r in ((lhs_high, rhs_high), (lhs_high, rhs_low), (lhs_low, rhs_high)):
                        for k in range(kc):
                            last = nc.tensor.matmul(outp, l[:, k, a], r[:, k, b], start=(n == 0), stop=(n == 3 * kc - 1))
                            n += 1
                    return last

                def body(i, q):
                    r = 1 - q
                    every = slice(None)
                    if alive(i):
                        pe.wait_ge(sg["xs_copied"], i + 1)
                        if after(i, 1):
                            pe.wait_ge(sg["th_in"], i)
                        for k in range(KC):
                            last = nc.tensor.transpose(m0[:, k * P:(k + 1) * P], xs[q][:, k, :], ident[:])
                        last.then_inc(sg["x_turned"], 1)
                    if alive(i - 1):
                        b = i - 1
                        if after(b, 1):
                            pe.wait_ge(sg["ot_in"], b)
                        for c in range(HC):
                            pe.wait_ge(sg["p_in"], 4 * b + c + 1)
                            for j in range(HQ):
                                hd = c * HQ + j
                                last = nc.tensor.matmul(m1[:, hd * W:(hd + 1) * W], e[r][:, c, j * S:(j + 1) * S],
                                                        kv[r][:, hd * W:(hd + 1) * W], start=True, stop=True)
                        last.then_inc(sg["bucket_in"], 1)
                    if alive(i - 2):
                        b = i - 2
                        pe.wait_ge(sg["ot_in"], b + 1)
                        if after(b, 1):
                            pe.wait_ge(sg["res_in"], b)
                        for k in range(KC):
                            last = nc.tensor.transpose(m2[:, k * P:(k + 1) * P], ot[q][:, k * P:(k + 1) * P], ident[:])
                        last.then_inc(sg["o_turned"], 1)
                    if alive(i):
                        pe.wait_ge(sg["n_in"], i + 1)
                        for k in range(KC):
                            last = nc.tensor.transpose(m0[:, D + k * P:D + (k + 1) * P], nt[q][:, k * P:(k + 1) * P],
                                                       ident[:])
                        last.then_inc(sg["n_turned"], 1)
                    if alive(i - 1):
                        b = i - 1
                        pe.wait_ge(sg["bk_in"], b + 1)
                        if after(b, 1):
                            pe.wait_ge(sg["qa_in"], b)
                        if alive(i) or isinstance(i, int):
                            pe.wait_ge(sg["kv_in"], b + 1)
                        for c in range(HC):
                            last = nc.tensor.transpose(m3[:, c * S:(c + 1) * S],
                                                       bk[r][:, c * HQ:(c + 1) * HQ, :].rearrange("p h w -> p (h w)"),
                                                       ident[:])
                        last.then_inc(sg["bk_turned"], 1)
                    if alive(i - 2):
                        b = i - 2
                        pe.wait_ge(sg["o_low"], b + 1)
                        three(m2[:, D:2 * D], every, every, oh[q], ol[q], wo_h, wo_l, KC).then_inc(sg["y_in"], 1)
                    if alive(i - 1):
                        b = i - 1
                        pe.wait_ge(sg["bkt_in"], b + 1)
                        for j in range(HQ):
                            if after(b, 1):
                                if j < 2:
                                    pe.wait_ge(sg["shifted"], 4 * b + j + 3)
                                else:
                                    pe.wait_ge(sg["et_in"], 4 * (b - 1) + j + 1)
                            elif j < 2:
                                pe.wait_ge(sg["shifted"], 4 * b + j + 3)
                            for c in range(HC):
                                last = nc.tensor.matmul(big[j][:, c * S:(c + 1) * S], qp[r][j * W:(j + 1) * W, c, :],
                                                        bkt[r][j * W:(j + 1) * W, c, :], start=True, stop=True)
                            last.then_inc(sg["s_in"], 1)
                    if alive(i):
                        pe.wait_ge(sg["n_low"], i + 1)
                        if alive(i - 1):
                            pe.wait_ge(sg["bv_in"], i)
                        for c in range(HC):
                            last = three(m1[:, c * T:(c + 1) * T], slice(c * P, (c + 1) * P), every, wq_h, wq_l,
                                         nh[q], nl[q], KC)
                        last.then_inc(sg["q_done"], 1)
                        pe.wait_ge(sg["xt_in"], i + 1)
                        for c in range(HC):
                            last = three(m0[:, c * T:(c + 1) * T], slice(c * P, (c + 1) * P), every, wp_h, wp_l,
                                         nh[q], nl[q], KC)
                        last.then_inc(sg["proj_done"], 1)
                        if alive(i - 1):
                            pe.wait_ge(sg["bkt_in"], i)
                        three(m3[:], every, every, nh[q], nl[q], wkv_h, wkv_l, KC).then_inc(sg["kv_done"], 1)

                    def logits(c):
                        bank = c % 2
                        if c < 2:
                            if alive(i - 1):
                                pe.wait_ge(sg["smax_in"], 4 * (i - 1) + c + 1)
                        else:
                            pe.wait_ge(sg["shifted"], 4 * i + c - 1)
                        nc.tensor.matmul(big[bank][:], th[q][:, c, :], protos[:], start=True, stop=True
                                         ).then_inc(sg["logits_in"], 1)

                    def scores_t(j):
                        b = i - 1
                        bank = 2 + j % 2
                        if j < 2:
                            pe.wait_ge(sg["smax_in"], 4 * b + j + 3)
                        else:
                            pe.wait_ge(sg["et_in"], 4 * b + j - 1)
                        for c in range(HC):
                            last = nc.tensor.matmul(big[bank][:, c * T:(c + 1) * T], bkt[r][j * W:(j + 1) * W, c, :],
                                                    qa[r][j * W:(j + 1) * W, c, :], start=True, stop=True)
                        last.then_inc(sg["st_in"], 1)

                    if alive(i):
                        pe.wait_ge(sg["th_in"], i + 1)
                        logits(0), logits(1)
                    if alive(i - 1):
                        b = i - 1
                        pe.wait_ge(sg["smax_in"], 4 * b + 4)
                        if alive(i):
                            pe.wait_ge(sg["kv_in"], i + 1)
                        for c in range(HC):
                            last = nc.tensor.transpose(m3[:, c * T:(c + 1) * T],
                                                       mp[r][:, c, :, :].rearrange("p j w -> p (j w)"), ident[:])
                        last.then_inc(sg["m_turned"], 1)
                        pe.wait_ge(sg["qa_in"], b + 1)
                        scores_t(0), scores_t(1)
                    if alive(i):
                        logits(2), logits(3)
                    if alive(i - 1):
                        scores_t(2), scores_t(3)
                    if alive(i - 2):
                        b = i - 2
                        pe.wait_ge(sg["h_in"], b + 1)
                        pe.wait_ge(sg["quant"], 7 * b + 7)
                        for k in range(KC):
                            last = nc.tensor.transpose(m2[:, k * P:(k + 1) * P], qv[q][:, k * P:(k + 1) * P], ident[:])
                        last.then_inc(sg["q_turned"], 1)
                    if alive(i - 1):
                        b = i - 1
                        if alive(i):
                            pe.wait_ge(sg["qp_in"], i + 1)
                        pe.wait_ge(sg["et_in"], 4 * b + 4)
                        for c in range(HC):
                            for j in range(HQ):
                                hd = c * HQ + j
                                last = nc.tensor.matmul(m1[:, hd * (HD + 1):(hd + 1) * (HD + 1)], pe_t[r][:, j, c, :],
                                                        bv[r][:, hd, :], start=True, stop=True)
                        last.then_inc(sg["pv_in"], 1)
                    if alive(i - 2):
                        b = i - 2
                        pe.wait_ge(sg["qt_in"], b + 1)
                        n = 0
                        for w in (wf_h, wf_l):
                            for k in range(KC):
                                last = nc.tensor.matmul(m2[:, D:2 * D], qt[q][:, k, :], w[:, k, :], start=(n == 0),
                                                        stop=(n == 3))
                                n += 1
                        last.then_inc(sg["f_in"], 1)

                pipeline(pe, body)


def build(nc, t, out, dims):
    SEQS, T, D, INNER, N, LAYERS, HEADS, TABLES, BITS = dims
    with ExitStack() as ctx:
        x_res = ctx.enter_context(nc.sbuf_tensor("x_res", [P, D // P, SEQS * T], F32))
        ident = ctx.enter_context(nc.sbuf_tensor("ident", [P, P], F32))
        tower_block(nc, t, x_res, ident, (SEQS, T, D, INNER, N, LAYERS))
        attention_block(nc, t, x_res, ident, out, (SEQS, T, D, HEADS, TABLES, BITS))


def kernel(**inputs):
    import numpy as np
    import concourse.bacc as bacc
    from concourse.bass_utils import run_bass_kernel_spmd

    a = {k.replace("L0_", ""): np.asarray(v) for k, v in inputs.items()}
    seqs, T = a["x"].shape
    layers, n, inner = a["tok_W_B"].shape
    d = a["tok_tok_emb"].shape[1]
    dim, heads = a["attn_planes_T"].shape[0], d // a["attn_planes_T"].shape[0]
    bits, protos = a["attn_protos_T"].shape
    tables = a["attn_planes_T"].shape[1] // bits
    mc, kc, w = inner // P, d // P, 32

    def rows(m):
        m = m.reshape(*m.shape[:-2], m.shape[-2] // P, P, m.shape[-1])
        return np.swapaxes(m, -3, -2)

    def per_channel(m):
        m = m.reshape(layers, -1, P, *m.shape[2:])
        return np.moveaxis(m, 2, 0).reshape(P, layers, -1)

    params = np.concatenate([per_channel(a["tok_conv_w"][:, :, 0, :]), per_channel(a["tok_conv_b"]),
                             per_channel(a["tok_D_vec"]), per_channel(a["tok_ln_g"]), per_channel(a["tok_ln_b"])], -1)
    wq = np.zeros((d, heads, w), np.float32)
    wq[:, :, :dim] = a["attn_Wq"].T.reshape(d, heads, dim)
    wkv = np.concatenate([a["attn_Wk"].T.reshape(d, heads, dim), a["attn_Wv"].T.reshape(d, heads, dim)], -1)
    arrays = {
        "tokens": a["x"].T, "tok_emb": a["tok_tok_emb"], "pos_emb": a["tok_pos_emb"], "params": params,
        "win": rows(np.swapaxes(a["tok_W_in"], 1, 2)), "wb": rows(np.swapaxes(a["tok_W_B"], 1, 2)),
        "wc": np.swapaxes(a["tok_W_C"], 1, 2), "wo": rows(np.swapaxes(a["tok_W_out"], 1, 2)),
        "wq": rows(wq.reshape(d, heads * w)), "wkv": rows(wkv.reshape(d, heads * w)), "wk_rows": rows(a["attn_Wk"]),
        "wo_attn": rows(a["attn_Wo"].T), "wf": rows(a["ffn_weight_fp8"].T), "bo": a["attn_bo"], "bias": a["ffn_bias"],
        "logit_temp": a["attn_logit_temp"].reshape(1), "input_scale": a["ffn_input_scale"],
        "weight_scale": a["ffn_weight_scale"], "planes": a["attn_planes_T"], "protos": a["attn_protos_T"],
    }
    nc = bacc.Bacc("TRN2", target_bir_lowering=False, num_devices=1)
    arrays = {f"in_{k}": np.ascontiguousarray(v) for k, v in arrays.items()}
    t = {k[3:]: nc.dram_tensor(k, v.shape, mybir.dt.from_np(v.dtype), kind="ExternalInput").ap()
         for k, v in arrays.items()}
    out = nc.dram_tensor("out", (seqs, T, d), F32, kind="ExternalOutput").ap()
    build(nc, t, out, (seqs, T, d, inner, n, layers, heads, tables, bits))
    r = run_bass_kernel_spmd(nc, [arrays], core_ids=[0])
    return r.results[0]["out"]
```

```python
from contextlib import ExitStack

import concourse.bass as bass
from concourse import mybir

ALU = mybir.AluOpType
ACT = mybir.ActivationFunctionType
F32 = mybir.dt.float32
F32R = mybir.dt.float32r
I32 = mybir.dt.int32
U32 = mybir.dt.uint32
AX = mybir.AxisListType

P = 128
DECAY, INP = 0.95, 0.05
EPS = 1e-5
FP8_MAX = 448.0
PAR = 28


def after(step, k):
    return not isinstance(step, int) or step >= k


def tower_block(nc, t, x_res, ident, dims):
    SEQS, T, D, INNER, N, LAYERS = dims
    KC = D // P
    MC = INNER // P
    GT = 4 * T
    G = SEQS * T // GT
    TS = GT // P
    SLOTS = 8

    with ExitStack() as ctx:
        def sb(name, shape, dt=F32):
            return ctx.enter_context(nc.sbuf_tensor(name, shape, dt))

        def ps(name, shape, dt=F32):
            return ctx.enter_context(nc.psum_tensor(name, shape, dt))

        def sem(name):
            return ctx.enter_context(nc.semaphore(name))

        idx = sb("idx", [P, SEQS], I32)
        pos = sb("pos", [P, D])
        decay = sb("decay", [P, GT])
        half_neg = sb("half_neg", [P, TS])
        par_all = sb("par_all", [P, LAYERS, PAR])
        par = sb("par", [P, PAR])
        win_raw = sb("win_raw", [P, KC, 2 * INNER])
        wb_raw = sb("wb_raw", [P, MC, N])
        wc_raw = sb("wc_raw", [P, INNER])
        wo_raw = sb("wo_raw", [P, MC, D])
        win_h = sb("win_h", [P, KC, 2 * INNER], F32R)
        win_l = sb("win_l", [P, KC, 2 * INNER], F32R)
        wb_hl = sb("wb_hl", [P, MC, 2 * N], F32R)
        wc_h = sb("wc_h", [P, INNER], F32R)
        wc_l = sb("wc_l", [P, INNER], F32R)
        wo_h = sb("wo_h", [P, MC, D], F32R)
        wo_l = sb("wo_l", [P, MC, D], F32R)
        xh = [sb(f"xh{i}", [P, KC, GT], F32R) for i in range(2)]
        xl = [sb(f"xl{i}", [P, KC, GT], F32R) for i in range(2)]
        u = [[sb(f"u{i}{m}", [P, GT]) for m in range(MC)] for i in range(2)]
        gates_sb = sb("gates_sb", [P, 2, MC, GT])
        gate = [[gates_sb[:, i, m, :] for m in range(MC)] for i in range(2)]
        emb = gates_sb[:, 0].rearrange("p m (a d) -> p (m a) d", d=D)
        uh = sb("uh", [P, MC, GT], F32R)
        ul = sb("ul", [P, MC, GT], F32R)
        yh = sb("yh", [P, MC, GT], F32R)
        yl = sb("yl", [P, MC, GT], F32R)
        hs = sb("hs", [P, GT])
        hs_h = sb("hs_h", [P, GT], F32R)
        hs_l = sb("hs_l", [P, GT], F32R)
        zstat = sb("zstat", [P, TS, 6])
        zmv = sb("zmv", [P, TS, 2])
        zvar = sb("zvar", [P, TS])
        zrstd = sb("zrstd", [P, TS])
        zn = sb("zn", [P, TS, D])
        ident_r = sb("ident_r", [P, P], F32R)

        proj = [ps(f"proj{i}", [P, GT]) for i in range(4)]
        bu = ps("bu", [P, GT])
        z = [ps(f"z{i}", [P, 2, D]) for i in range(2)]
        zt = ps("zt", [P, GT])

        consts_loaded = sem("consts_loaded")
        consts_made = sem("consts_made")
        ident_zeroed = sem("ident_zeroed")
        gathered = [sem(f"gathered{j}") for j in range(SLOTS)]
        pos_added = sem("pos_added")
        emb_turned = sem("emb_turned")
        x_ready = sem("x_ready")
        raw_loaded = sem("raw_loaded")
        w_high = sem("w_high")
        w_split = sem("w_split")
        par_ready = sem("par_ready")
        x_high = sem("x_high")
        x_low = sem("x_low")
        in_proj = sem("in_proj")
        tap0 = sem("tap0")
        conv_tap = sem("conv_tap")
        gated = sem("gated")
        u_high = sem("u_high")
        u_full = sem("u_full")
        u_low = sem("u_low")
        bu_done = sem("bu_done")
        scanned = sem("scanned")
        hs_high = sem("hs_high")
        hs_low = sem("hs_low")
        hc_done = sem("hc_done")
        y_taken = sem("y_taken")
        y_full = sem("y_full")
        y_high = sem("y_high")
        y_low = sem("y_low")
        residual_in = sem("residual_in")
        z_done = sem("z_done")
        z_stat = sem("z_stat")
        z_mv = sem("z_mv")
        z_var = sem("z_var")
        z_rstd = sem("z_rstd")
        z_normed = sem("z_normed")
        z_turned = sem("z_turned")

        def pipeline(eng, body):
            for i in range(4):
                body(i, i % 2)
            with eng.Fori(2, G // 2 - 1) as pair:
                body(2 * pair, 0)
                body(2 * pair + 1, 1)
            for i in range(G - 2, G + 2):
                body(i, i % 2)

        def alive(g):
            return not isinstance(g, int) or 0 <= g < G

        with nc.Block() as block:

            @block.sync
            def _(sp):
                sp.dma_start(idx[:], t["tokens"]).then_inc(consts_loaded, 16)
                sp.dma_start(pos[:], t["pos_emb"][0:T, :]).then_inc(consts_loaded, 16)
                sp.dma_start(par_all[:], t["params"]).then_inc(consts_loaded, 16)
                def load_weights(layer):
                    for raw, name in ((win_raw, "win"), (wb_raw, "wb"), (wo_raw, "wo")):
                        sp.dma_start(raw[:], t[name][layer]).then_inc(raw_loaded, 16)
                    for half in range(2):
                        sp.dma_start(wc_raw[half * N:(half + 1) * N, :], t["wc"][layer]).then_inc(raw_loaded, 16)

                load_weights(0)
                with sp.Fori(1, LAYERS) as layer:
                    sp.wait_ge(w_split, 4 * layer)
                    load_weights(layer)

            @block.gpsimd
            def _(pool):
                nc.gpsimd.memset(half_neg[:], -0.5).then_inc(consts_made, 1)
                nc.gpsimd.memset(ident[:], 0.0).then_inc(ident_zeroed, 1)
                pool.wait_ge(ident_zeroed, 1)
                nc.gpsimd.affine_select(out=ident[:], in_=ident[:], compare_op=ALU.not_equal, fill=1.0, base=0,
                                        pattern=[[-1, P]], channel_multiplier=1).then_inc(consts_made, 1)
                pool.wait_ge(consts_loaded, 48)
                for n in range(SEQS):
                    if n >= SLOTS and n % 2 == 0:
                        pool.wait_ge(emb_turned, (n - SLOTS) // 2 + 1)
                    nc.gpsimd.indirect_dma_start(
                        emb[:, n % SLOTS, :], None, t["tok_emb"], bass.IndirectOffsetOnAxis(ap=idx[:, n:n + 1], axis=0),
                    ).then_inc(gathered[n % SLOTS], 16)

                def split_x(g, par_, s):
                    pool.wait_ge(x_high, s + 1)
                    nc.gpsimd.tensor_tensor(xl[par_][:], x_res[:, :, bass.ds(g * GT, GT)],
                                            xh[par_][:].bitcast(F32), ALU.subtract).then_inc(x_low, 1)

                def u_lows(g, q, s, ms):
                    for m in ms:
                        pool.wait_ge(u_full, 4 * s + m + 1)
                        if after(g, 1) and m == ms[0]:
                            pool.wait_ge(bu_done, s)
                        nc.gpsimd.tensor_tensor(ul[:, m, :], u[q][m][:], uh[:, m, :].bitcast(F32),
                                                ALU.subtract).then_inc(u_low, 1)

                with pool.Fori(0, LAYERS) as layer:
                    split_x(0, 0, layer * G)

                    def body(i, q):
                        s = layer * G + i
                        if alive(i):
                            u_lows(i, q, s, (0, 1))
                        if alive(i - 1):
                            for m in range(MC):
                                pool.wait_ge(y_high, 4 * (s - 1) + m + 1)
                                nc.gpsimd.tensor_tensor(yl[:, m, :], u[1 - q][m][:], yh[:, m, :].bitcast(F32),
                                                        ALU.subtract).then_inc(y_low, 1)
                        if alive(i):
                            u_lows(i, q, s, (2, 3))
                        if alive(i + 1):
                            split_x(i + 1, 1 - q, s + 1)
                        if alive(i - 1):
                            for t_ in range(TS // 2):
                                pool.wait_ge(z_var, 2 * (s - 1) + t_ + 1)
                                nc.gpsimd.tensor_tensor(zrstd[:, 2 * t_:2 * t_ + 2], zvar[:, 2 * t_:2 * t_ + 2],
                                                        half_neg[:, 0:2], ALU.pow).then_inc(z_rstd, 1)

                    pipeline(pool, body)

            @block.scalar
            def _(act):
                with act.Fori(0, SEQS // 4) as r:
                    for q in range(2):
                        act.wait_ge(emb_turned, 2 * r + q + 1)
                        nc.scalar.activation(x_res[:, :, bass.ds((2 * r + q) * 2 * T, 2 * T)],
                                             proj[q][:].rearrange("p (k t) -> p k t", k=KC),
                                             ACT.Copy).then_inc(x_ready, 1)

                with act.Fori(0, LAYERS) as layer:
                    act.wait_ge(raw_loaded, 80 * (layer + 1))
                    nc.scalar.activation(win_h[:], win_raw[:], ACT.Copy).then_inc(w_high, 1)
                    nc.scalar.activation(wb_hl[:, :, 0:N], wb_raw[:], ACT.Copy).then_inc(w_high, 1)
                    nc.scalar.activation(wc_h[:], wc_raw[:], ACT.Copy, scale=INP).then_inc(w_high, 1)
                    nc.scalar.activation(wo_h[:], wo_raw[:], ACT.Copy).then_inc(w_high, 1)
                    act.wait_ge(par_ready, layer + 1)

                    def body(i, q):
                        s = layer * G + i

                        def tap(m):
                            act.wait_ge(in_proj, 8 * s + 2 * m + 1)
                            nc.scalar.activation(u[q][m][:], proj[2 * (m % 2)][:], ACT.Identity,
                                                 bias=par[:, 16 + m:17 + m], scale=par[:, 4 * m + 3:4 * m + 4],
                                                 ).then_inc(tap0, 1)

                        def gates(m):
                            act.wait_ge(in_proj, 8 * s + 2 * m + 2)
                            nc.scalar.activation(gate[q][m], proj[2 * (m % 2) + 1][:], ACT.Silu).then_inc(gated, 1)

                        def silu(m):
                            act.wait_ge(conv_tap, 12 * s + 3 * m + 3)
                            if after(i, 1) and m == 0:
                                act.wait_ge(bu_done, s)
                            nc.scalar.activation(uh[:, m, :], u[q][m][:], ACT.Silu).then_inc(u_high, 1)
                            nc.scalar.activation(u[q][m][:], u[q][m][:], ACT.Silu).then_inc(u_full, 1)

                        if alive(i):
                            tap(0), gates(0), tap(1), gates(1), silu(0), silu(1)
                        if alive(i - 1):
                            for m in range(MC):
                                act.wait_ge(y_full, 4 * (s - 1) + m + 1)
                                nc.scalar.activation(yh[:, m, :], u[1 - q][m][:], ACT.Copy).then_inc(y_high, 1)

                        def finish(k):
                            act.wait_ge(z_turned, 2 * (s - 2) + k + 1)
                            nc.scalar.activation(x_res[:, k, bass.ds((i - 2) * GT, GT)], zt[:], ACT.Identity,
                                                 bias=par[:, 26 + k:27 + k], scale=par[:, 24 + k:25 + k],
                                                 ).then_inc(x_ready, 1)

                        if alive(i):
                            tap(2), gates(2), tap(3), gates(3)
                        if alive(i - 2):
                            finish(0)
                        if alive(i):
                            silu(2)
                        if alive(i - 2):
                            finish(1)
                        if alive(i):
                            silu(3)

                    pipeline(act, body)

            @block.vector
            def _(dve):
                nc.vector.memset(decay[:], DECAY).then_inc(consts_made, 1)
                dve.wait_ge(consts_made, 3)
                nc.vector.memset(decay[:].rearrange("p (s t) -> p s t", t=T)[:, :, 0:1], 0.0).then_inc(consts_made, 1)
                nc.vector.tensor_copy(ident_r[:], ident[:]).then_inc(consts_made, 1)
                dve.wait_ge(consts_loaded, 48)
                dve.wait_ge(consts_made, 5)
                with dve.Fori(0, SEQS // SLOTS) as r:
                    for j in range(SLOTS):
                        dve.wait_ge(gathered[j], 16 * r + 16)
                        nc.vector.tensor_tensor(emb[:, j, :], emb[:, j, :], pos[:], ALU.add).then_inc(pos_added, 1)

                def split_x(g, q, s):
                    dve.wait_ge(x_ready, 2 * s + 2)
                    nc.vector.tensor_copy(xh[q][:], x_res[:, :, bass.ds(g * GT, GT)]).then_inc(x_high, 1)

                with dve.Fori(0, LAYERS) as layer:
                    dve.wait_ge(x_ready, 2 * G * (layer + 1))
                    nc.vector.tensor_copy(par[:], par_all[:, bass.ds(layer, 1), :]).then_inc(par_ready, 1)
                    split_x(0, 0, layer * G)
                    dve.wait_ge(w_high, 4 * layer + 1)
                    nc.vector.tensor_tensor(win_l[:], win_raw[:], win_h[:].bitcast(F32), ALU.subtract).then_inc(w_split, 1)
                    dve.wait_ge(w_high, 4 * layer + 4)
                    nc.vector.tensor_tensor(wb_hl[:, :, N:2 * N], wb_raw[:], wb_hl[:, :, 0:N].bitcast(F32),
                                            ALU.subtract).then_inc(w_split, 1)
                    nc.vector.scalar_tensor_tensor(wc_l[:], wc_raw[:], INP, wc_h[:].bitcast(F32), ALU.mult,
                                                   ALU.subtract).then_inc(w_split, 1)
                    nc.vector.tensor_tensor(wo_l[:], wo_raw[:], wo_h[:].bitcast(F32), ALU.subtract).then_inc(w_split, 1)
                    dve.wait_ge(par_ready, layer + 1)

                    def body(i, q):
                        s = layer * G + i

                        def conv(m):
                            dve.wait_ge(tap0, 4 * s + m + 1)
                            src = proj[2 * (m % 2)][:].rearrange("p (s t) -> p s t", t=T)
                            dst = u[q][m][:].rearrange("p (s t) -> p s t", t=T)
                            for n in range(1, 4):
                                if n > 1:
                                    dve.wait_ge(conv_tap, 12 * s + 3 * m + n - 1)
                                nc.vector.scalar_tensor_tensor(
                                    dst[:, :, n:T], src[:, :, 0:T - n], par[:, 4 * m + 3 - n:4 * m + 4 - n],
                                    dst[:, :, n:T], ALU.mult, ALU.add).then_inc(conv_tap, 1)

                        if alive(i):
                            conv(0), conv(1)
                        if alive(i - 1):
                            for m in range(MC):
                                dve.wait_ge(hc_done, 4 * (s - 1) + m + 1)
                                nc.vector.scalar_tensor_tensor(u[1 - q][m][:], u[1 - q][m][:], par[:, 20 + m:21 + m],
                                                               proj[m][:], ALU.mult, ALU.add).then_inc(y_taken, 1)
                                dve.wait_ge(y_taken, 4 * (s - 1) + m + 1)
                                nc.vector.tensor_tensor(u[1 - q][m][:], u[1 - q][m][:], gate[1 - q][m], ALU.mult
                                                        ).then_inc(y_full, 1)
                        if alive(i):
                            conv(2), conv(3)
                        if alive(i + 1):
                            if alive(i - 1):
                                dve.wait_ge(residual_in, s)
                            split_x(i + 1, 1 - q, s + 1)
                        if alive(i - 1):
                            for k in range(TS):
                                dve.wait_ge(z_done, 2 * (s - 1) + k // 2 + 1)
                                nc.vector.bn_stats(zstat[:, k, :], z[k // 2][:, k % 2, :]).then_inc(z_stat, 1)
                                dve.wait_ge(consts_made, 5)
                                dve.wait_ge(z_stat, 4 * (s - 1) + k + 1)
                                nc.vector.bn_aggr(zmv[:, k, :], zstat[:, k, :]).then_inc(z_mv, 1)
                                if k % 2:
                                    dve.wait_ge(z_mv, 4 * (s - 1) + k + 1)
                                    nc.vector.tensor_scalar(zvar[:, k - 1:k + 1], zmv[:, k - 1:k + 1, 1], EPS, None,
                                                            ALU.add).then_inc(z_var, 1)
                        if alive(i):
                            dve.wait_ge(bu_done, s + 1)
                            nc.vector.tensor_tensor_scan(hs[:], decay[:], bu[:], 0.0, ALU.mult, ALU.add
                                                         ).then_inc(scanned, 1)
                            dve.wait_ge(scanned, s + 1)
                            nc.vector.tensor_copy(hs_h[:], hs[:]).then_inc(hs_high, 1)
                            dve.wait_ge(hs_high, s + 1)
                            nc.vector.tensor_tensor(hs_l[:], hs[:], hs_h[:].bitcast(F32), ALU.subtract
                                                    ).then_inc(hs_low, 1)
                        if alive(i - 1):
                            if after(i - 1, 1):
                                dve.wait_ge(z_turned, 2 * (s - 1))
                            for k in range(TS):
                                dve.wait_ge(z_rstd, 2 * (s - 1) + k // 2 + 1)
                                nc.vector.tensor_scalar(zn[:, k, :], z[k // 2][:, k % 2, :], zmv[:, k, 0:1],
                                                        zrstd[:, k:k + 1], ALU.subtract, ALU.mult
                                                        ).then_inc(z_normed, 1)

                    pipeline(dve, body)

            @block.tensor
            def _(pe):
                pe.wait_ge(consts_made, 5)
                def turn_rows(r):
                    for j in range(SLOTS):
                        pair = j // 2
                        pe.wait_ge(pos_added, r * SLOTS + j + 1)
                        if j % 2 == 0 and (after(r, 1) or pair >= 2):
                            pe.wait_ge(x_ready, (SLOTS // 2) * r + pair - 1)
                        for k in range(KC):
                            last = nc.tensor.transpose(
                                proj[pair % 2][:, k * 2 * T + (j % 2) * T:k * 2 * T + (j % 2) * T + T],
                                emb[:, j, k * P:(k + 1) * P], ident[:])
                        if j % 2:
                            last.then_inc(emb_turned, 1)

                turn_rows(0)
                with pe.Fori(1, SEQS // SLOTS) as r:
                    turn_rows(r)

                with pe.Fori(0, LAYERS) as layer:
                    def body(i, q):
                        s = layer * G + i

                        def in_unit(m, is_gate):
                            bank = proj[2 * (m % 2) + is_gate]
                            if m < 2:
                                if after(i, 1):
                                    if is_gate:
                                        pe.wait_ge(gated, 4 * (s - 1) + m + 3)
                                    else:
                                        pe.wait_ge(conv_tap, 12 * (s - 1) + 3 * (m + 2) + 3)
                            elif after(i, 1):
                                pe.wait_ge(y_taken, 4 * (s - 1) + 2 * (m - 2) + is_gate + 1)
                            elif is_gate:
                                pe.wait_ge(gated, 4 * s + m - 1)
                            else:
                                pe.wait_ge(conv_tap, 12 * s + 3 * (m - 2) + 3)
                            c = is_gate * INNER + m * P
                            n = 0
                            for w, x in ((win_h, xh), (win_h, xl), (win_l, xh)):
                                for k in range(KC):
                                    last = nc.tensor.matmul(bank[:], w[:, k, c:c + P], x[q][:, k, :],
                                                            start=(n == 0), stop=(n == 5))
                                    n += 1
                            last.then_inc(in_proj, 1)

                        if alive(i):
                            pe.wait_ge(w_split, 4 * layer + 4)
                            pe.wait_ge(x_low, s + 1)
                            for m in range(2):
                                in_unit(m, 0), in_unit(m, 1)
                        if alive(i - 1):
                            pe.wait_ge(hs_low, s)
                            for m in range(MC):
                                if alive(i):
                                    if m % 2:
                                        pe.wait_ge(gated, 4 * s + m // 2 + 1)
                                    else:
                                        pe.wait_ge(conv_tap, 12 * s + 3 * (m // 2) + 3)
                                for n, (w, h) in enumerate(((wc_h, hs_h), (wc_h, hs_l), (wc_l, hs_h))):
                                    last = nc.tensor.matmul(proj[m][:], w[:, m * P:(m + 1) * P], h[:],
                                                            start=(n == 0), stop=(n == 2))
                                last.then_inc(hc_done, 1)
                        if alive(i):
                            for m in range(2, MC):
                                in_unit(m, 0), in_unit(m, 1)
                        def turn_back(k):
                            pe.wait_ge(z_normed, 4 * (s - 1))
                            if k:
                                pe.wait_ge(x_ready, 2 * G + 2 * (s - 2) + k)
                            elif after(i - 2, 1):
                                pe.wait_ge(x_ready, 2 * G + 2 * (s - 2))
                            for j in range(TS):
                                last = nc.tensor.transpose(zt[:, j * P:(j + 1) * P], zn[:, j, k * P:(k + 1) * P],
                                                           ident[:])
                            last.then_inc(z_turned, 1)

                        if alive(i - 2):
                            turn_back(0)
                        if alive(i - 1):
                            if after(i - 1, 1):
                                pe.wait_ge(z_normed, 4 * (s - 1))
                            for j in range(TS):
                                for k in range(KC):
                                    for n, x in enumerate((xh, xl)):
                                        last = nc.tensor.matmul(
                                            z[j // 2][:, j % 2, k * P:(k + 1) * P], x[1 - q][:, k, j * P:(j + 1) * P],
                                            ident_r[:], start=(j % 2 == 0 and k == 0 and n == 0), stop=False,
                                            skip_group_check=True)
                            last.then_inc(residual_in, 1)
                        if alive(i - 2):
                            turn_back(1)
                        if alive(i - 1):
                            pe.wait_ge(y_low, 4 * s)
                            for j in range(TS):
                                for m in range(MC):
                                    for n, (a, w) in enumerate(((yh, wo_h), (yh, wo_l), (yl, wo_h))):
                                        last = nc.tensor.matmul(
                                            z[j // 2][:, j % 2, :], a[:, m, j * P:(j + 1) * P], w[:, m, :],
                                            start=False, stop=(m == MC - 1 and n == 2), skip_group_check=True)
                                if j % 2:
                                    last.then_inc(z_done, 1)
                        if alive(i):
                            if after(i, 1):
                                pe.wait_ge(scanned, s)
                            for m in range(MC):
                                pe.wait_ge(u_low, 4 * s + m + 1)
                                nc.tensor.matmul(bu[:], wb_hl[:, m, :], uh[:, m, :], start=(m == 0), stop=False)
                                last = nc.tensor.matmul(bu[:], wb_hl[:, m, :], ul[:, m, :], start=False,
                                                        stop=(m == MC - 1))
                            last.then_inc(bu_done, 1)

                    pipeline(pe, body)


def attention_block(nc, t, x_res, ident, out, dims):
    SEQS, T, D, HEADS, TABLES, BITS = dims
    HD = D // HEADS
    R = 1 << BITS
    S = TABLES * R
    KC = D // P
    HC = 4
    HQ = HEADS // HC
    W = P // HQ
    UNROLL = 4

    with ExitStack() as ctx:
        def sb(name, shape, dt=F32):
            return ctx.enter_context(nc.sbuf_tensor(name, shape, dt))

        def two(name, shape, dt=F32):
            return [sb(f"{name}{i}", shape, dt) for i in range(2)]

        def ps(name, shape, dt=F32):
            return ctx.enter_context(nc.psum_tensor(name, shape, dt))

        def sem(name):
            return ctx.enter_context(nc.semaphore(name))

        e2 = two("e2", [P, HQ, HC, S])
        raw, wkv_raw = (tile[:, 0:2].rearrange("p (k a) c s -> p k (a c s)", k=KC) for tile in e2)
        wq_h, wq_l = sb("wq_h", [P, KC, HEADS * W], F32R), sb("wq_l", [P, KC, HEADS * W], F32R)
        wkv_h, wkv_l = sb("wkv_h", [P, KC, HEADS * W], F32R), sb("wkv_l", [P, KC, HEADS * W], F32R)
        wp_h, wp_l = sb("wp_h", [P, KC, HEADS * W], F32R), sb("wp_l", [P, KC, HEADS * W], F32R)
        protos = sb("protos", [P, HQ * S])
        planes = sb("planes", [P, P // HD * W])
        wo_h, wo_l = sb("awo_h", [P, HC, D], F32R), sb("awo_l", [P, HC, D], F32R)
        wf_h, wf_l = sb("wf_h", [P, KC, D], F32R), sb("wf_l", [P, KC, D], F32R)
        bo = sb("bo", [P, D])
        bias = sb("bias", [P, D])
        scal = sb("scal", [P, 8])
        half_neg = sb("ahalf_neg", [P, 1])
        xs = two("xs", [P, KC, T])
        stat, mv, var, rstd = sb("stat", [P, 6]), sb("mv", [P, 2]), sb("var", [P, 1]), sb("rstd", [P, 1])
        nt = two("nt", [P, D])
        nh, nl = sb("nh", [P, KC, 2, T], F32R), sb("nl", [P, KC, 2, T], F32R)
        th = sb("th", [P, 2, HC, T])
        qp = sb("qp", [P, UNROLL, HC, T])
        kv = sb("kv", [P, UNROLL, HEADS * W])
        lmax = sb("lmax", [P, HC, HQ * TABLES])
        e = two("e", [P, HC, HQ * S])
        lsum = sb("lsum", [P, HC, HQ * TABLES])
        lrec = two("lrec", [P, HC, HQ * TABLES])
        bkt = sb("bkt", [P, HC, S])
        bkv = two("bkv", [P, HEADS * W])
        nmx = sb("nmx", [P, HQ, HC])
        ssum = sb("ssum", [P, HQ, HC])
        srec = sb("srec", [P, HQ, HC])
        pe_t = sb("pe_t", [P, HQ, HC, T])
        wo_raw = pe_t[:, 0:2].rearrange("p a c t -> p (a c t)").rearrange("p (c d) -> p c d", d=D)
        oh, ol = sb("oh", [P, HC, T], F32R), sb("ol", [P, HC, T], F32R)
        wk_rows = pe_t[:, 2:3].rearrange("p a c t -> p (a c t)").rearrange("p (k d) -> p k d", d=D)
        wf_raw = pe_t[:, 3:4].rearrange("p a c t -> p (a c t)").rearrange("p (k d) -> p k d", d=D)
        xb = two("xb", [P, KC, T])
        h = sb("h", [P, D])
        hb = sb("hb", [P, D])
        stat2, mv2, var2, rstd2 = sb("stat2", [P, 6]), sb("mv2", [P, 2]), sb("var2", [P, 1]), sb("rstd2", [P, 1])
        v = sb("v", [P, D])
        ulp = sb("ulp", [P, D])
        qv = sb("qv", [P, D])
        qt = sb("qt", [P, KC, T], F32R)
        res = two("res", [P, D])

        big = [ps(f"big{i}", [P, 512]) for i in range(4)]
        rows_bank, even_bank, odd_bank, back_bank = (
            ps(name, [P, 512]) for name in ("rows_bank", "even_bank", "odd_bank", "back_bank"))

        names = """loaded zeroed made scales blocks raw_high w_done wp_in
            xs_copied x_turned stat_in mv_in var_in rstd_in n_in n_turned n_high n_low
            proj_done th_in q_done qp_in kv_done kv_in logits_in lmax_in shifted e_in lsum_in lrec_in p_in
            bucket_in bkt_in bkv_turned bkv_in s_in smax_in es_in srec_in share_in
            es_turned et_in o_in o_high o_low
            xb_copied y_in h_in hb_in stat2_in mv2_in var2_in rstd2_in quant q_turned qt_in f_in res_in""".split()
        sg = {n: sem("a_" + n) for n in names}
        out_sent = [sem(f"out_sent{i}") for i in range(2)]

        def alive(b):
            return not isinstance(b, int) or 0 <= b < SEQS

        def pipeline(eng, body):
            for i in range(-2, UNROLL):
                body(i, i % UNROLL)
            with eng.Fori(1, SEQS // UNROLL - 1) as quad:
                for u in range(UNROLL):
                    body(UNROLL * quad + u, u)
            for i in range(SEQS - UNROLL, SEQS + 3):
                body(i, i % UNROLL)

        with nc.Block() as block:

            @block.sync
            def _(sp):
                sp.dma_start(raw[:], t["wq"]).then_inc(sg["loaded"], 16)
                sp.dma_start(wkv_raw[:], t["wkv"]).then_inc(sg["loaded"], 16)
                sp.dma_start(wk_rows[:], t["wk_rows"]).then_inc(sg["loaded"], 16)
                sp.dma_start(wo_raw[:], t["wo_attn"]).then_inc(sg["loaded"], 16)
                sp.dma_start(wf_raw[:], t["wf"]).then_inc(sg["loaded"], 16)
                for tile, name in ((bo, "bo"), (bias, "bias")):
                    sp.dma_start(tile[:], t[name].partition_broadcast(P)).then_inc(sg["loaded"], 16)
                for c, name in enumerate(("logit_temp", "input_scale", "weight_scale")):
                    sp.dma_start(scal[:, c:c + 1], t[name].partition_broadcast(P)).then_inc(sg["loaded"], 16)
                sp.wait_ge(sg["zeroed"], 2)
                for j in range(P // HD):
                    sp.dma_start(planes[j * HD:(j + 1) * HD, j * W:(j + 1) * W], t["planes"]).then_inc(sg["blocks"], 16)
                for j in range(HQ * TABLES):
                    sp.dma_start(protos[j * BITS:(j + 1) * BITS, j * R:(j + 1) * R], t["protos"]
                                 ).then_inc(sg["blocks"], 16)

                def body(i, u):
                    b, q = i - 3, (u + 1) % 2
                    if alive(b):
                        sp.wait_ge(sg["res_in"], b + 1)
                        sp.dma_start(out[bass.ds(b, 1), :, :].rearrange("b t d -> t (b d)"), res[q][:]
                                     ).then_inc(out_sent[q], 16)
                pipeline(sp, body)
                for q in range(2):
                    sp.wait_ge(out_sent[q], 16 * (SEQS // 2))

            @block.gpsimd
            def _(pool):
                nc.gpsimd.memset(planes[:], 0.0).then_inc(sg["zeroed"], 1)
                nc.gpsimd.memset(protos[:], 0.0).then_inc(sg["zeroed"], 1)
                nc.gpsimd.memset(half_neg[:], -0.5).then_inc(sg["made"], 1)
                pool.wait_ge(sg["made"], 1)
                pool.wait_ge(sg["loaded"], 160)

                def copy_rows(b, q):
                    if after(b, 2):
                        pool.wait_ge(sg["x_turned"], b - 1)
                    nc.gpsimd.tensor_copy(xs[q][:], x_res[:, :, bass.ds(b * T, T)]).then_inc(sg["xs_copied"], 1)

                copy_rows(0, 0)

                def body(i, u):
                    q = u % 2
                    if alive(i - 2):
                        pool.wait_ge(sg["srec_in"], i - 1)
                        for j in range(HQ):
                            nc.gpsimd.tensor_tensor(e2[q][:, j], e2[q][:, j],
                                                    srec[:, j, :].unsqueeze(2).broadcast_to([P, HC, S]), ALU.mult
                                                    ).then_inc(sg["share_in"], 1)
                    if alive(i - 3):
                        pool.wait_ge(sg["var2_in"], i - 2)
                        nc.gpsimd.tensor_tensor(rstd2[:], var2[:], half_neg[:], ALU.pow).then_inc(sg["rstd2_in"], 1)

                    def table_share(c):
                        pool.wait_ge(sg["lrec_in"], 4 * i + c + 1)
                        ev = e[q][:, c, :].rearrange("p (a r) -> p a r", r=R)
                        rv = lrec[q][:, c, :].unsqueeze(2).broadcast_to([P, HQ * TABLES, R])
                        nc.gpsimd.tensor_tensor(ev, ev, rv, ALU.mult).then_inc(sg["p_in"], 1)

                    if alive(i):
                        table_share(0)
                    if alive(i + 2):
                        pool.wait_ge(sg["var_in"], i + 3)
                        nc.gpsimd.tensor_tensor(rstd[:], var[:], half_neg[:], ALU.pow).then_inc(sg["rstd_in"], 1)
                    if alive(i):
                        table_share(1)
                    if alive(i - 3):
                        b = i - 3
                        pool.wait_ge(sg["h_in"], b + 1)
                        if after(b, 1):
                            pool.wait_ge(sg["res_in"], b)
                        nc.gpsimd.tensor_tensor(hb[:], h[:], bias[:], ALU.add).then_inc(sg["hb_in"], 1)
                    if alive(i):
                        table_share(2), table_share(3)
                    if alive(i - 2):
                        if after(i, 4):
                            pool.wait_ge(sg["y_in"], i - 3)
                        nc.gpsimd.tensor_copy(xb[q][:], x_res[:, :, bass.ds((i - 2) * T, T)]).then_inc(sg["xb_copied"], 1)
                    if alive(i + 3):
                        copy_rows(i + 3, 1 - q)

                pipeline(pool, body)

            @block.scalar
            def _(act):
                act.wait_ge(sg["loaded"], 160)
                nc.scalar.activation(scal[:, 3:4], scal[:, 0:1], ACT.Exp).then_inc(sg["raw_high"], 1)
                nc.scalar.activation(wq_h[:], raw[:], ACT.Identity, scale=HD ** -0.5).then_inc(sg["raw_high"], 1)
                nc.scalar.activation(wkv_h[:], wkv_raw[:], ACT.Copy).then_inc(sg["raw_high"], 1)
                nc.scalar.activation(wo_h[:], wo_raw[:], ACT.Copy).then_inc(sg["raw_high"], 1)
                act.wait_ge(sg["w_done"], 1)
                nc.scalar.activation(wf_h[:], wf_raw[:], ACT.Copy).then_inc(sg["raw_high"], 1)
                for k in range(KC):
                    act.wait_ge(sg["wp_in"], k + 1)
                    nc.scalar.activation(wp_h[:, k, :], big[k][:], ACT.Copy).then_inc(sg["raw_high"], 1)

                def body(i, u):
                    q, r = u % 2, 1 - u % 2
                    banks = (even_bank, odd_bank)
                    if u % 2 == 0 and alive(i):
                        pairs = [bank[:].rearrange("p (c s t) -> p s c t", c=2, s=2) for bank in banks]
                        for half in range(2):
                            act.wait_ge(sg["proj_done"], i + half + 1)
                            nc.scalar.activation(th[:, :, 2 * half:2 * half + 2, :], pairs[half], ACT.Tanh
                                                 ).then_inc(sg["th_in"], 1)
                        for half in range(2):
                            act.wait_ge(sg["q_done"], i + half + 1)
                            nc.scalar.activation(qp[:, u:u + 2, 2 * half:2 * half + 2, :], pairs[half], ACT.Copy
                                                 ).then_inc(sg["qp_in"], 1)
                        for s in range(2):
                            act.wait_ge(sg["kv_done"], i + s + 1)
                            nc.scalar.activation(kv[:, u + s, :], banks[s][:], ACT.Copy).then_inc(sg["kv_in"], 1)
                    if alive(i - 1):
                        act.wait_ge(sg["bucket_in"], i)
                        nc.scalar.activation(bkt[:], even_bank[:].rearrange("p (c s) -> p c s", c=HC), ACT.Copy
                                             ).then_inc(sg["bkt_in"], 1)

                    def exp_logits(c):
                        act.wait_ge(sg["shifted"], 4 * i + c + 1)
                        nc.scalar.activation(e[q][:, c, :], e[q][:, c, :], ACT.Exp).then_inc(sg["e_in"], 1)

                    def take_turned(j):
                        act.wait_ge(sg["es_turned"], 4 * (i - 2) + j + 1)
                        nc.scalar.activation(pe_t[:, j], banks[1 - j % 2][:].rearrange("p (c t) -> p c t", c=HC),
                                             ACT.Copy).then_inc(sg["et_in"], 1)

                    def exp_scores(j):
                        act.wait_ge(sg["smax_in"], 4 * (i - 1) + j + 1)
                        for c in range(HC):
                            last = nc.scalar.activation(e2[r][:, j, c, :], big[j][:, c * S:(c + 1) * S], ACT.Exp,
                                                        bias=nmx[:, j, c:c + 1], accum_out=ssum[:, j, c:c + 1])
                        last.then_inc(sg["es_in"], 1)

                    if alive(i):
                        exp_logits(0)
                    if alive(i - 1):
                        act.wait_ge(sg["bkv_turned"], i)
                        nc.scalar.activation(bkv[r][:], even_bank[:], ACT.Copy).then_inc(sg["bkv_in"], 1)
                    if alive(i):
                        exp_logits(1)
                    if alive(i - 2):
                        take_turned(0)
                    if alive(i):
                        exp_logits(2)
                    if alive(i - 2):
                        take_turned(1)
                    if alive(i):
                        exp_logits(3)
                    for j in range(HQ):
                        if j < 2 and alive(i - 2):
                            take_turned(2 + j)
                        if alive(i - 1):
                            exp_scores(j)
                    if alive(i + 2):
                        act.wait_ge(sg["n_turned"], i + 3)
                        nc.scalar.activation(nh[:, :, q, :], rows_bank[:, D:2 * D].rearrange("p (k t) -> p k t", k=KC),
                                             ACT.Copy).then_inc(sg["n_high"], 1)
                    if alive(i - 2):
                        act.wait_ge(sg["o_in"], i - 1)
                        nc.scalar.activation(oh[:], odd_bank[:].rearrange("p (c t) -> p c t", c=HC), ACT.Copy
                                             ).then_inc(sg["o_high"], 1)
                    if alive(i - 3):
                        act.wait_ge(sg["q_turned"], i - 2)
                        nc.scalar.activation(qt[:], back_bank[:, 0:D].rearrange("p (k t) -> p k t", k=KC), ACT.Copy
                                             ).then_inc(sg["qt_in"], 1)

                pipeline(act, body)

            @block.vector
            def _(dve):
                dve.wait_ge(sg["raw_high"], 1)
                nc.vector.tensor_scalar(scal[:, 3:4], scal[:, 3:4], 0.01, 20.0, ALU.max, ALU.min).then_inc(sg["scales"], 1)
                nc.vector.tensor_tensor(scal[:, 5:6], scal[:, 1:2], scal[:, 2:3], ALU.mult).then_inc(sg["scales"], 1)
                nc.vector.reciprocal(scal[:, 6:7], scal[:, 1:2]).then_inc(sg["scales"], 1)
                dve.wait_ge(sg["scales"], 3)
                nc.vector.reciprocal(scal[:, 4:5], scal[:, 3:4]).then_inc(sg["scales"], 1)
                nc.vector.tensor_scalar(wf_raw[:], wf_raw[:], scal[:, 5:6], None, ALU.mult).then_inc(sg["w_done"], 1)
                dve.wait_ge(sg["scales"], 4)
                dve.wait_ge(sg["blocks"], 16 * (P // HD + HQ * TABLES))
                nc.vector.tensor_scalar(protos[:], protos[:], scal[:, 4:5], None, ALU.mult).then_inc(sg["w_done"], 1)
                dve.wait_ge(sg["raw_high"], 7)
                dve.wait_ge(sg["w_done"], 2)
                nc.vector.scalar_tensor_tensor(wq_l[:], raw[:], HD ** -0.5, wq_h[:].bitcast(F32), ALU.mult, ALU.subtract
                                               ).then_inc(sg["w_done"], 1)
                for lo, full, hi in ((wkv_l, wkv_raw, wkv_h), (wo_l, wo_raw, wo_h), (wf_l, wf_raw, wf_h)):
                    nc.vector.tensor_tensor(lo[:], full[:], hi[:].bitcast(F32), ALU.subtract).then_inc(sg["w_done"], 1)
                for k in range(KC):
                    nc.vector.tensor_tensor(wp_l[:, k, :], big[k][:], wp_h[:, k, :].bitcast(F32), ALU.subtract
                                            ).then_inc(sg["w_done"], 1)

                def body(i, u):
                    q = u % 2

                    def shift(c):
                        bank = big[c][:].rearrange("p (a r) -> p a r", r=R)
                        dve.wait_ge(sg["logits_in"], 4 * i + c + 1)
                        nc.vector.tensor_reduce(lmax[:, c, :], bank, AX.X, ALU.max).then_inc(sg["lmax_in"], 1)
                        dve.wait_ge(sg["lmax_in"], 4 * i + c + 1)
                        nc.vector.tensor_tensor(e[q][:, c, :].rearrange("p (a r) -> p a r", r=R), bank,
                                                lmax[:, c, :].unsqueeze(2).broadcast_to([P, HQ * TABLES, R]),
                                                ALU.subtract).then_inc(sg["shifted"], 1)

                    def total(c):
                        dve.wait_ge(sg["e_in"], 4 * i + c + 1)
                        nc.vector.tensor_reduce(lsum[:, c, :], e[q][:, c, :].rearrange("p (a r) -> p a r", r=R),
                                                AX.X, ALU.add).then_inc(sg["lsum_in"], 1)
                        dve.wait_ge(sg["lsum_in"], 4 * i + c + 1)
                        nc.vector.reciprocal(lrec[q][:, c, :], lsum[:, c, :]).then_inc(sg["lrec_in"], 1)

                    def most(j):
                        dve.wait_ge(sg["s_in"], 4 * (i - 1) + j + 1)
                        nc.vector.tensor_reduce(nmx[:, j, :], big[j][:].rearrange("p (c s) -> p c s", c=HC),
                                                AX.X, ALU.max, negate=True).then_inc(sg["smax_in"], 1)

                    if alive(i - 2):
                        dve.wait_ge(sg["es_in"], 4 * (i - 2) + 4)
                        nc.vector.reciprocal(srec[:], ssum[:]).then_inc(sg["srec_in"], 1)
                    if alive(i - 3):
                        b = i - 3
                        dve.wait_ge(sg["y_in"], b + 1)
                        if after(b, 1):
                            dve.wait_ge(sg["hb_in"], b)
                        nc.vector.tensor_tensor(h[:], back_bank[:, D:2 * D], bo[:], ALU.add).then_inc(sg["h_in"], 1)
                        dve.wait_ge(sg["h_in"], b + 1)
                        nc.vector.bn_stats(stat2[:], h[:]).then_inc(sg["stat2_in"], 1)
                        dve.wait_ge(sg["w_done"], 2)
                        dve.wait_ge(sg["stat2_in"], b + 1)
                        nc.vector.bn_aggr(mv2[:], stat2[:]).then_inc(sg["mv2_in"], 1)
                        dve.wait_ge(sg["mv2_in"], b + 1)
                        nc.vector.tensor_scalar(var2[:], mv2[:, 1:2], EPS, None, ALU.add).then_inc(sg["var2_in"], 1)
                    if alive(i):
                        shift(0), shift(1), shift(2), shift(3)
                    if alive(i + 2):
                        dve.wait_ge(sg["x_turned"], i + 3)
                        nc.vector.bn_stats(stat[:], rows_bank[:, 0:D]).then_inc(sg["stat_in"], 1)
                        dve.wait_ge(sg["w_done"], 2)
                        dve.wait_ge(sg["stat_in"], i + 3)
                        nc.vector.bn_aggr(mv[:], stat[:]).then_inc(sg["mv_in"], 1)
                        dve.wait_ge(sg["mv_in"], i + 3)
                        nc.vector.tensor_scalar(var[:], mv[:, 1:2], EPS, None, ALU.add).then_inc(sg["var_in"], 1)
                    for j in range(HQ):
                        if alive(i):
                            total(j)
                        if alive(i - 1):
                            most(j)
                    if alive(i + 2):
                        dve.wait_ge(sg["rstd_in"], i + 3)
                        nc.vector.tensor_scalar(nt[q][:], rows_bank[:, 0:D], mv[:, 0:1], rstd[:, 0:1], ALU.subtract,
                                                ALU.mult).then_inc(sg["n_in"], 1)
                    if alive(i - 3):
                        b = i - 3
                        step = [0]

                        def chain(ins):
                            step[0] += 1
                            ins.then_inc(sg["quant"], 1)
                            dve.wait_ge(sg["quant"], 7 * b + step[0])

                        dve.wait_ge(sg["rstd2_in"], b + 1)
                        chain(nc.vector.tensor_scalar(v[:], h[:], mv2[:, 0:1], rstd2[:, 0:1], ALU.subtract, ALU.mult))
                        chain(nc.vector.tensor_scalar(v[:], v[:], scal[:, 6:7], FP8_MAX, ALU.mult, ALU.min))
                        chain(nc.vector.tensor_scalar(v[:], v[:], -FP8_MAX, None, ALU.max))
                        chain(nc.vector.tensor_scalar(ulp[:].bitcast(U32), v[:].bitcast(U32), 0x7F800000, None,
                                                      ALU.bitwise_and))
                        chain(nc.vector.tensor_scalar(ulp[:], ulp[:], 2.0 ** -6, 1.5 * 2.0 ** 20, ALU.max, ALU.mult))
                        chain(nc.vector.tensor_tensor(v[:], v[:], ulp[:], ALU.add))
                        if after(b, 1):
                            dve.wait_ge(sg["q_turned"], b)
                        chain(nc.vector.tensor_tensor(qv[:], v[:], ulp[:], ALU.subtract))
                    if alive(i + 2):
                        dve.wait_ge(sg["n_high"], i + 3)
                        nc.vector.tensor_tensor(nl[:, :, q, :], rows_bank[:, D:2 * D].rearrange("p (k t) -> p k t", k=KC),
                                                nh[:, :, q, :].bitcast(F32), ALU.subtract).then_inc(sg["n_low"], 1)
                    if alive(i - 2):
                        dve.wait_ge(sg["o_high"], i - 1)
                        nc.vector.tensor_tensor(ol[:], odd_bank[:].rearrange("p (c t) -> p c t", c=HC),
                                                oh[:].bitcast(F32), ALU.subtract).then_inc(sg["o_low"], 1)
                    if alive(i - 3):
                        b = i - 3
                        dve.wait_ge(sg["f_in"], b + 1)
                        dve.wait_ge(sg["hb_in"], b + 1)
                        if after(b, 2):
                            dve.wait_ge(out_sent[1 - q], 8 * (b - (1 - q)))
                        nc.vector.tensor_tensor(res[1 - q][:], back_bank[:, D:2 * D], hb[:], ALU.add
                                                ).then_inc(sg["res_in"], 1)

                pipeline(dve, body)

            @block.tensor
            def _(pe):
                pe.wait_ge(sg["loaded"], 160)
                pe.wait_ge(sg["blocks"], 16 * (P // HD + HQ * TABLES))
                for k in range(KC):
                    for c in range(KC):
                        last = nc.tensor.matmul(big[k][:, c * 256:(c + 1) * 256], wk_rows[:, c, k * P:(k + 1) * P],
                                                planes[:], start=True, stop=True)
                    last.then_inc(sg["wp_in"], 1)
                pe.wait_ge(sg["w_done"], 8)

                def three(outp, high, low, rhs_high, rhs_low, chunks, final=True):
                    n = 0
                    for l, r in ((high, rhs_high), (high, rhs_low), (low, rhs_high)):
                        for k in range(chunks):
                            last = nc.tensor.matmul(outp, l(k), r(k), start=(n == 0),
                                                    stop=(final and n == 3 * chunks - 1), skip_group_check=True)
                            n += 1
                    return last

                def body(i, u):
                    q, r = u % 2, 1 - u % 2
                    banks = (even_bank, odd_bank)
                    if u % 2 == 0 and alive(i):
                        pe.wait_ge(sg["n_low"], i + 2)
                        for name, high, low in (("proj_done", wp_h, wp_l), ("q_done", wq_h, wq_l)):
                            for half in range(2):
                                if name == "q_done":
                                    pe.wait_ge(sg["th_in"], i + half + 1)
                                elif half and after(i, 3):
                                    pe.wait_ge(sg["o_low"], i - 2)
                                for c in (2 * half, 2 * half + 1):
                                    cut = slice(c * P, (c + 1) * P)
                                    last = three(banks[half][:, c % 2 * 2 * T:(c % 2 + 1) * 2 * T],
                                                 lambda k: high[:, k, cut], lambda k: low[:, k, cut],
                                                 lambda k: nh[:, k].rearrange("p s t -> p (s t)"),
                                                 lambda k: nl[:, k].rearrange("p s t -> p (s t)"), KC)
                                last.then_inc(sg[name], 1)
                        for s in range(2):
                            pe.wait_ge(sg["qp_in"], i + s + 1)
                            three(banks[s][:], lambda k: nh[:, k, s, :], lambda k: nl[:, k, s, :],
                                  lambda k: wkv_h[:, k, :], lambda k: wkv_l[:, k, :], KC).then_inc(sg["kv_done"], 1)
                    if alive(i - 1):
                        b = i - 1
                        if u % 2 == 0 and alive(i):
                            pe.wait_ge(sg["kv_in"], i + 1)
                        for c in range(HC):
                            pe.wait_ge(sg["p_in"], 4 * b + c + 1)
                            for j in range(HQ):
                                hd = c * HQ + j
                                last = nc.tensor.matmul(even_bank[j * W:(j + 1) * W, c * S:(c + 1) * S],
                                                        kv[:, (u - 1) % UNROLL, hd * W:(hd + 1) * W],
                                                        e[r][:, c, j * S:(j + 1) * S], start=True, stop=True)
                        last.then_inc(sg["bucket_in"], 1)
                    if alive(i - 3):
                        b = i - 3
                        pe.wait_ge(sg["o_low"], b + 1)
                        if after(b, 1):
                            pe.wait_ge(sg["res_in"], b)
                        three(back_bank[:, D:2 * D], lambda k: oh[:, k, :], lambda k: ol[:, k, :],
                              lambda k: wo_h[:, k, :], lambda k: wo_l[:, k, :], HC, final=False)
                        pe.wait_ge(sg["xb_copied"], b + 1)
                        for k in range(KC):
                            last = nc.tensor.matmul(back_bank[:, D + k * P:D + (k + 1) * P], xb[r][:, k, :], ident[:],
                                                    start=False, stop=(k == KC - 1), skip_group_check=True)
                        last.then_inc(sg["y_in"], 1)
                    if alive(i):
                        pe.wait_ge(sg["th_in"], i + 2 - q)
                        for c in range(HC):
                            if alive(i - 2):
                                pe.wait_ge(sg["es_in"], 4 * (i - 2) + c + 1)
                            elif i == 1:
                                pe.wait_ge(sg["shifted"], c + 1)
                            nc.tensor.matmul(big[c][:], th[:, q, c, :], protos[:], start=True, stop=True
                                             ).then_inc(sg["logits_in"], 1)
                    if alive(i + 2):
                        pe.wait_ge(sg["xs_copied"], i + 3)
                        if after(i + 2, 1):
                            pe.wait_ge(sg["n_low"], i + 2)
                        for k in range(KC):
                            last = nc.tensor.transpose(rows_bank[:, k * P:(k + 1) * P], xs[q][:, k, :], ident[:])
                        last.then_inc(sg["x_turned"], 1)
                    if alive(i - 1):
                        pe.wait_ge(sg["bkt_in"], i)
                        for c in range(HC):
                            last = nc.tensor.transpose(even_bank[:, c * P:(c + 1) * P], bkt[:, c, :], ident[:])
                        last.then_inc(sg["bkv_turned"], 1)

                    def turn_scores(j):
                        b = i - 2
                        if j == 0:
                            if u % 2 == 0 and alive(i):
                                pe.wait_ge(sg["kv_in"], i + 2)
                            elif alive(i - 3):
                                pe.wait_ge(sg["o_low"], i - 2)
                        elif j == 1:
                            if alive(i - 1):
                                pe.wait_ge(sg["bkv_in"], i)
                        else:
                            pe.wait_ge(sg["et_in"], 4 * b + j - 1)
                        pe.wait_ge(sg["share_in"], 4 * b + j + 1)
                        for c in range(HC):
                            last = nc.tensor.transpose(banks[1 - j % 2][:, c * T:(c + 1) * T], e2[q][:, j, c, :],
                                                       ident[:])
                        last.then_inc(sg["es_turned"], 1)

                    def scores(j):
                        if alive(i):
                            pe.wait_ge(sg["shifted"], 4 * i + j + 1)
                        elif alive(i - 2):
                            pe.wait_ge(sg["es_in"], 4 * (i - 2) + j + 1)
                        for c in range(HC):
                            last = nc.tensor.matmul(big[j][:, c * S:(c + 1) * S],
                                                    qp[j * W:(j + 1) * W, (u - 1) % UNROLL, c, :],
                                                    bkt[j * W:(j + 1) * W, c, :], start=True, stop=True)
                        last.then_inc(sg["s_in"], 1)

                    for j in range(HQ):
                        if alive(i - 2):
                            turn_scores(j)
                        if alive(i - 1):
                            scores(j)
                    if alive(i + 2):
                        pe.wait_ge(sg["n_in"], i + 3)
                        for k in range(KC):
                            last = nc.tensor.transpose(rows_bank[:, D + k * P:D + (k + 1) * P],
                                                       nt[q][:, k * P:(k + 1) * P], ident[:])
                        last.then_inc(sg["n_turned"], 1)
                    if alive(i - 2):
                        b = i - 2
                        for j in range(HQ):
                            pe.wait_ge(sg["et_in"], 4 * b + 4)
                            for c in range(HC):
                                hd = c * HQ + j
                                last = nc.tensor.matmul(odd_bank[j * W:(j + 1) * W, c * T:(c + 1) * T],
                                                        bkv[q][:, hd * W:(hd + 1) * W], pe_t[:, j, c, :],
                                                        start=True, stop=True)
                        last.then_inc(sg["o_in"], 1)
                    if alive(i - 3):
                        b = i - 3
                        pe.wait_ge(sg["quant"], 7 * b + 7)
                        for k in range(KC):
                            last = nc.tensor.transpose(back_bank[:, k * P:(k + 1) * P], qv[:, k * P:(k + 1) * P],
                                                       ident[:])
                        last.then_inc(sg["q_turned"], 1)
                        pe.wait_ge(sg["qt_in"], b + 1)
                        n = 0
                        for w in (wf_h, wf_l):
                            for k in range(KC):
                                last = nc.tensor.matmul(back_bank[:, D:2 * D], qt[:, k, :], w[:, k, :], start=(n == 0),
                                                        stop=(n == 3))
                                n += 1
                        last.then_inc(sg["f_in"], 1)

                pipeline(pe, body)


def build(nc, t, out, dims):
    SEQS, T, D, INNER, N, LAYERS, HEADS, TABLES, BITS = dims
    with ExitStack() as ctx:
        x_res = ctx.enter_context(nc.sbuf_tensor("x_res", [P, D // P, SEQS * T], F32))
        ident = ctx.enter_context(nc.sbuf_tensor("ident", [P, P], F32))
        tower_block(nc, t, x_res, ident, (SEQS, T, D, INNER, N, LAYERS))
        attention_block(nc, t, x_res, ident, out, (SEQS, T, D, HEADS, TABLES, BITS))


def kernel(**inputs):
    import numpy as np
    import concourse.bacc as bacc
    from concourse.bass_utils import run_bass_kernel_spmd

    a = {k.replace("L0_", ""): np.asarray(v) for k, v in inputs.items()}
    seqs, T = a["x"].shape
    layers, n, inner = a["tok_W_B"].shape
    d = a["tok_tok_emb"].shape[1]
    dim, heads = a["attn_planes_T"].shape[0], d // a["attn_planes_T"].shape[0]
    bits, protos = a["attn_protos_T"].shape
    tables = a["attn_planes_T"].shape[1] // bits
    mc, kc, w = inner // P, d // P, 32

    def rows(m):
        m = m.reshape(*m.shape[:-2], m.shape[-2] // P, P, m.shape[-1])
        return np.swapaxes(m, -3, -2)

    def per_channel(m):
        m = m.reshape(layers, -1, P, *m.shape[2:])
        return np.moveaxis(m, 2, 0).reshape(P, layers, -1)

    params = np.concatenate([per_channel(a["tok_conv_w"][:, :, 0, :]), per_channel(a["tok_conv_b"]),
                             per_channel(a["tok_D_vec"]), per_channel(a["tok_ln_g"]), per_channel(a["tok_ln_b"])], -1)
    wq = np.zeros((d, heads, w), np.float32)
    wq[:, :, :dim] = a["attn_Wq"].T.reshape(d, heads, dim)
    wo = np.zeros((heads, w, d), np.float32)
    wo[:, dim:] = a["attn_Wo"].T.reshape(heads, dim, d)
    wkv = np.concatenate([a["attn_Wk"].T.reshape(d, heads, dim), a["attn_Wv"].T.reshape(d, heads, dim)], -1)
    arrays = {
        "tokens": a["x"].T, "tok_emb": a["tok_tok_emb"], "pos_emb": a["tok_pos_emb"], "params": params,
        "win": rows(np.swapaxes(a["tok_W_in"], 1, 2)), "wb": rows(np.swapaxes(a["tok_W_B"], 1, 2)),
        "wc": np.swapaxes(a["tok_W_C"], 1, 2), "wo": rows(np.swapaxes(a["tok_W_out"], 1, 2)),
        "wq": rows(wq.reshape(d, heads * w)), "wkv": rows(wkv.reshape(d, heads * w)), "wk_rows": rows(a["attn_Wk"]),
        "wo_attn": rows(wo.reshape(heads * w, d)), "wf": rows(a["ffn_weight_fp8"].T), "bo": a["attn_bo"], "bias": a["ffn_bias"],
        "logit_temp": a["attn_logit_temp"].reshape(1), "input_scale": a["ffn_input_scale"],
        "weight_scale": a["ffn_weight_scale"], "planes": a["attn_planes_T"], "protos": a["attn_protos_T"],
    }
    nc = bacc.Bacc("TRN2", target_bir_lowering=False, num_devices=1)
    arrays = {f"in_{k}": np.ascontiguousarray(v) for k, v in arrays.items()}
    t = {k[3:]: nc.dram_tensor(k, v.shape, mybir.dt.from_np(v.dtype), kind="ExternalInput").ap()
         for k, v in arrays.items()}
    out = nc.dram_tensor("out", (seqs, T, d), F32, kind="ExternalOutput").ap()
    build(nc, t, out, (seqs, T, d, inner, n, layers, heads, tables, bits))
    r = run_bass_kernel_spmd(nc, [arrays], core_ids=[0])
    return r.results[0]["out"]
```

```python
from contextlib import ExitStack

import concourse.bass as bass
from concourse import mybir

ALU = mybir.AluOpType
ACT = mybir.ActivationFunctionType
F32 = mybir.dt.float32
F32R = mybir.dt.float32r
I32 = mybir.dt.int32
U32 = mybir.dt.uint32
AX = mybir.AxisListType

P = 128
DECAY, INP = 0.95, 0.05
EPS = 1e-5
FP8_MAX = 448.0
PAR = 28


def after(step, k):
    return not isinstance(step, int) or step >= k


def tower_block(nc, t, x_res, ident, dims):
    SEQS, T, D, INNER, N, LAYERS = dims
    KC = D // P
    MC = INNER // P
    GT = 4 * T
    G = SEQS * T // GT
    TS = GT // P
    SLOTS = 8

    with ExitStack() as ctx:
        def sb(name, shape, dt=F32):
            return ctx.enter_context(nc.sbuf_tensor(name, shape, dt))

        def ps(name, shape, dt=F32):
            return ctx.enter_context(nc.psum_tensor(name, shape, dt))

        def sem(name):
            return ctx.enter_context(nc.semaphore(name))

        idx = sb("idx", [P, SEQS], I32)
        pos = sb("pos", [P, D])
        decay = sb("decay", [P, GT])
        half_neg = sb("half_neg", [P, TS])
        par_all = sb("par_all", [P, LAYERS, PAR])
        par = sb("par", [P, PAR])
        win_raw = sb("win_raw", [P, KC, 2 * INNER])
        wb_raw = sb("wb_raw", [P, MC, N])
        wc_raw = sb("wc_raw", [P, INNER])
        wo_raw = sb("wo_raw", [P, MC, D])
        win_h = sb("win_h", [P, KC, 2 * INNER], F32R)
        win_l = sb("win_l", [P, KC, 2 * INNER], F32R)
        wb_hl = sb("wb_hl", [P, MC, 2 * N], F32R)
        wc_h = sb("wc_h", [P, INNER], F32R)
        wc_l = sb("wc_l", [P, INNER], F32R)
        wo_h = sb("wo_h", [P, MC, D], F32R)
        wo_l = sb("wo_l", [P, MC, D], F32R)
        xh = [sb(f"xh{i}", [P, KC, GT], F32R) for i in range(2)]
        xl = [sb(f"xl{i}", [P, KC, GT], F32R) for i in range(2)]
        u = [[sb(f"u{i}{m}", [P, GT]) for m in range(MC)] for i in range(2)]
        gates_sb = sb("gates_sb", [P, 2, MC, GT])
        gate = [[gates_sb[:, i, m, :] for m in range(MC)] for i in range(2)]
        emb = gates_sb[:, 0].rearrange("p m (a d) -> p (m a) d", d=D)
        uh = sb("uh", [P, MC, GT], F32R)
        ul = sb("ul", [P, MC, GT], F32R)
        yh = sb("yh", [P, MC, GT], F32R)
        yl = sb("yl", [P, MC, GT], F32R)
        hs = sb("hs", [P, GT])
        hs_h = sb("hs_h", [P, GT], F32R)
        hs_l = sb("hs_l", [P, GT], F32R)
        zstat = sb("zstat", [P, TS, 6])
        zmv = sb("zmv", [P, TS, 2])
        zvar = sb("zvar", [P, TS])
        zrstd = sb("zrstd", [P, TS])
        zn = sb("zn", [P, TS, D])
        ident_r = sb("ident_r", [P, P], F32R)

        proj = [ps(f"proj{i}", [P, GT]) for i in range(4)]
        bu = ps("bu", [P, GT])
        z = [ps(f"z{i}", [P, 2, D]) for i in range(2)]
        zt = ps("zt", [P, GT])

        consts_loaded = sem("consts_loaded")
        consts_made = sem("consts_made")
        ident_zeroed = sem("ident_zeroed")
        gathered = [sem(f"gathered{j}") for j in range(SLOTS)]
        pos_added = sem("pos_added")
        emb_turned = sem("emb_turned")
        x_ready = sem("x_ready")
        raw_loaded = sem("raw_loaded")
        w_high = sem("w_high")
        w_split = sem("w_split")
        par_ready = sem("par_ready")
        x_high = sem("x_high")
        x_low = sem("x_low")
        in_proj = sem("in_proj")
        tap0 = sem("tap0")
        conv_tap = sem("conv_tap")
        gated = sem("gated")
        u_high = sem("u_high")
        u_full = sem("u_full")
        u_low = sem("u_low")
        bu_done = sem("bu_done")
        scanned = sem("scanned")
        hs_high = sem("hs_high")
        hs_low = sem("hs_low")
        hc_done = sem("hc_done")
        y_taken = sem("y_taken")
        y_full = sem("y_full")
        y_high = sem("y_high")
        y_low = sem("y_low")
        residual_in = sem("residual_in")
        z_done = sem("z_done")
        z_stat = sem("z_stat")
        z_mv = sem("z_mv")
        z_var = sem("z_var")
        z_rstd = sem("z_rstd")
        z_normed = sem("z_normed")
        z_turned = sem("z_turned")

        Y_ORDER = (0, 1, 3, 2)
        IN_ORDER = ((0, 0), (0, 1), (1, 0), (1, 1), (2, 0), (2, 1), (3, 1), (3, 0))

        def pipeline(eng, body):
            for i in range(4):
                body(i, i % 2)
            with eng.Fori(2, G // 2 - 1) as pair:
                body(2 * pair, 0)
                body(2 * pair + 1, 1)
            for i in range(G - 2, G + 2):
                body(i, i % 2)

        def alive(g):
            return not isinstance(g, int) or 0 <= g < G

        with nc.Block() as block:

            @block.sync
            def _(sp):
                sp.dma_start(idx[:], t["tokens"]).then_inc(consts_loaded, 16)
                sp.dma_start(pos[:], t["pos_emb"][0:T, :]).then_inc(consts_loaded, 16)
                sp.dma_start(par_all[:], t["params"]).then_inc(consts_loaded, 16)
                def load_weights(layer):
                    for raw, name in ((win_raw, "win"), (wb_raw, "wb"), (wo_raw, "wo")):
                        sp.dma_start(raw[:], t[name][layer]).then_inc(raw_loaded, 16)
                    for half in range(2):
                        sp.dma_start(wc_raw[half * N:(half + 1) * N, :], t["wc"][layer]).then_inc(raw_loaded, 16)

                load_weights(0)
                with sp.Fori(1, LAYERS) as layer:
                    sp.wait_ge(w_split, 4 * layer)
                    load_weights(layer)

            @block.gpsimd
            def _(pool):
                nc.gpsimd.memset(half_neg[:], -0.5).then_inc(consts_made, 1)
                nc.gpsimd.memset(ident[:], 0.0).then_inc(ident_zeroed, 1)
                pool.wait_ge(ident_zeroed, 1)
                nc.gpsimd.affine_select(out=ident[:], in_=ident[:], compare_op=ALU.not_equal, fill=1.0, base=0,
                                        pattern=[[-1, P]], channel_multiplier=1).then_inc(consts_made, 1)
                pool.wait_ge(consts_loaded, 48)
                for n in range(SEQS):
                    if n >= SLOTS and n % 2 == 0:
                        pool.wait_ge(emb_turned, (n - SLOTS) // 2 + 1)
                    nc.gpsimd.indirect_dma_start(
                        emb[:, n % SLOTS, :], None, t["tok_emb"], bass.IndirectOffsetOnAxis(ap=idx[:, n:n + 1], axis=0),
                    ).then_inc(gathered[n % SLOTS], 16)

                def split_x(g, par_, s):
                    pool.wait_ge(x_high, s + 1)
                    nc.gpsimd.tensor_tensor(xl[par_][:], x_res[:, :, bass.ds(g * GT, GT)],
                                            xh[par_][:].bitcast(F32), ALU.subtract).then_inc(x_low, 1)

                def u_lows(g, q, s, ms):
                    for m in ms:
                        pool.wait_ge(u_full, 4 * s + m + 1)
                        if after(g, 1) and m == ms[0]:
                            pool.wait_ge(bu_done, s)
                        nc.gpsimd.tensor_tensor(ul[:, m, :], u[q][m][:], uh[:, m, :].bitcast(F32),
                                                ALU.subtract).then_inc(u_low, 1)

                with pool.Fori(0, LAYERS) as layer:
                    split_x(0, 0, layer * G)

                    def body(i, q):
                        s = layer * G + i
                        if alive(i):
                            u_lows(i, q, s, (0, 1))
                        if alive(i - 1):
                            for n, m in enumerate(Y_ORDER):
                                pool.wait_ge(y_high, 4 * (s - 1) + n + 1)
                                nc.gpsimd.tensor_tensor(yl[:, m, :], u[1 - q][m][:], yh[:, m, :].bitcast(F32),
                                                        ALU.subtract).then_inc(y_low, 1)
                        if alive(i):
                            u_lows(i, q, s, (2, 3))
                        if alive(i + 1):
                            split_x(i + 1, 1 - q, s + 1)
                        if alive(i - 1):
                            for t_ in range(TS // 2):
                                pool.wait_ge(z_var, 2 * (s - 1) + t_ + 1)
                                nc.gpsimd.tensor_tensor(zrstd[:, 2 * t_:2 * t_ + 2], zvar[:, 2 * t_:2 * t_ + 2],
                                                        half_neg[:, 0:2], ALU.pow).then_inc(z_rstd, 1)

                    pipeline(pool, body)

            @block.scalar
            def _(act):
                with act.Fori(0, SEQS // 4) as r:
                    for q in range(2):
                        act.wait_ge(emb_turned, 2 * r + q + 1)
                        nc.scalar.activation(x_res[:, :, bass.ds((2 * r + q) * 2 * T, 2 * T)],
                                             proj[q][:].rearrange("p (k t) -> p k t", k=KC),
                                             ACT.Copy).then_inc(x_ready, 1)

                with act.Fori(0, LAYERS) as layer:
                    act.wait_ge(raw_loaded, 80 * (layer + 1))
                    nc.scalar.activation(win_h[:], win_raw[:], ACT.Copy).then_inc(w_high, 1)
                    nc.scalar.activation(wb_hl[:, :, 0:N], wb_raw[:], ACT.Copy).then_inc(w_high, 1)
                    nc.scalar.activation(wc_h[:], wc_raw[:], ACT.Copy, scale=INP).then_inc(w_high, 1)
                    nc.scalar.activation(wo_h[:], wo_raw[:], ACT.Copy).then_inc(w_high, 1)
                    act.wait_ge(par_ready, layer + 1)

                    def body(i, q):
                        s = layer * G + i

                        def tap(m):
                            act.wait_ge(in_proj, 8 * s + IN_ORDER.index((m, 0)) + 1)
                            nc.scalar.activation(u[q][m][:], proj[2 * (m % 2)][:], ACT.Identity,
                                                 bias=par[:, 16 + m:17 + m], scale=par[:, 4 * m + 3:4 * m + 4],
                                                 ).then_inc(tap0, 1)

                        def gates(m):
                            act.wait_ge(in_proj, 8 * s + IN_ORDER.index((m, 1)) + 1)
                            nc.scalar.activation(gate[q][m], proj[2 * (m % 2) + 1][:], ACT.Silu).then_inc(gated, 1)

                        def silu(m):
                            act.wait_ge(conv_tap, 12 * s + 3 * m + 3)
                            if after(i, 1) and m == 0:
                                act.wait_ge(bu_done, s)
                            nc.scalar.activation(uh[:, m, :], u[q][m][:], ACT.Silu).then_inc(u_high, 1)
                            nc.scalar.activation(u[q][m][:], u[q][m][:], ACT.Silu).then_inc(u_full, 1)

                        if alive(i):
                            tap(0), gates(0), tap(1), gates(1), silu(0), silu(1)
                        if alive(i - 1):
                            for n, m in enumerate(Y_ORDER):
                                act.wait_ge(y_full, 4 * (s - 1) + n + 1)
                                nc.scalar.activation(yh[:, m, :], u[1 - q][m][:], ACT.Copy).then_inc(y_high, 1)

                        def finish(k):
                            act.wait_ge(z_turned, 2 * (s - 2) + k + 1)
                            nc.scalar.activation(x_res[:, k, bass.ds((i - 2) * GT, GT)], zt[:], ACT.Identity,
                                                 bias=par[:, 26 + k:27 + k], scale=par[:, 24 + k:25 + k],
                                                 ).then_inc(x_ready, 1)

                        if alive(i):
                            tap(2), gates(2), gates(3), tap(3)
                        if alive(i - 2):
                            finish(0)
                        if alive(i):
                            silu(2), silu(3)
                        if alive(i - 2):
                            finish(1)

                    pipeline(act, body)

            @block.vector
            def _(dve):
                nc.vector.memset(decay[:], DECAY).then_inc(consts_made, 1)
                dve.wait_ge(consts_made, 3)
                nc.vector.memset(decay[:].rearrange("p (s t) -> p s t", t=T)[:, :, 0:1], 0.0).then_inc(consts_made, 1)
                nc.vector.tensor_copy(ident_r[:], ident[:]).then_inc(consts_made, 1)
                dve.wait_ge(consts_loaded, 48)
                dve.wait_ge(consts_made, 5)
                with dve.Fori(0, SEQS // SLOTS) as r:
                    for j in range(SLOTS):
                        dve.wait_ge(gathered[j], 16 * r + 16)
                        nc.vector.tensor_tensor(emb[:, j, :], emb[:, j, :], pos[:], ALU.add).then_inc(pos_added, 1)

                def split_x(g, q, s):
                    dve.wait_ge(x_ready, 2 * s + 2)
                    nc.vector.tensor_copy(xh[q][:], x_res[:, :, bass.ds(g * GT, GT)]).then_inc(x_high, 1)

                with dve.Fori(0, LAYERS) as layer:
                    dve.wait_ge(x_ready, 2 * G * (layer + 1))
                    nc.vector.tensor_copy(par[:], par_all[:, bass.ds(layer, 1), :]).then_inc(par_ready, 1)
                    split_x(0, 0, layer * G)
                    dve.wait_ge(w_high, 4 * layer + 1)
                    nc.vector.tensor_tensor(win_l[:], win_raw[:], win_h[:].bitcast(F32), ALU.subtract).then_inc(w_split, 1)
                    dve.wait_ge(w_high, 4 * layer + 4)
                    nc.vector.tensor_tensor(wb_hl[:, :, N:2 * N], wb_raw[:], wb_hl[:, :, 0:N].bitcast(F32),
                                            ALU.subtract).then_inc(w_split, 1)
                    nc.vector.scalar_tensor_tensor(wc_l[:], wc_raw[:], INP, wc_h[:].bitcast(F32), ALU.mult,
                                                   ALU.subtract).then_inc(w_split, 1)
                    nc.vector.tensor_tensor(wo_l[:], wo_raw[:], wo_h[:].bitcast(F32), ALU.subtract).then_inc(w_split, 1)
                    dve.wait_ge(par_ready, layer + 1)

                    def body(i, q):
                        s = layer * G + i

                        def conv(m):
                            dve.wait_ge(tap0, 4 * s + m + 1)
                            src = proj[2 * (m % 2)][:].rearrange("p (s t) -> p s t", t=T)
                            dst = u[q][m][:].rearrange("p (s t) -> p s t", t=T)
                            for n in range(1, 4):
                                if n > 1:
                                    dve.wait_ge(conv_tap, 12 * s + 3 * m + n - 1)
                                nc.vector.scalar_tensor_tensor(
                                    dst[:, :, n:T], src[:, :, 0:T - n], par[:, 4 * m + 3 - n:4 * m + 4 - n],
                                    dst[:, :, n:T], ALU.mult, ALU.add).then_inc(conv_tap, 1)

                        if alive(i):
                            conv(0), conv(1)
                        if alive(i - 1):
                            for n, m in enumerate(Y_ORDER):
                                dve.wait_ge(hc_done, 4 * (s - 1) + n + 1)
                                nc.vector.scalar_tensor_tensor(u[1 - q][m][:], u[1 - q][m][:], par[:, 20 + m:21 + m],
                                                               proj[m][:], ALU.mult, ALU.add).then_inc(y_taken, 1)
                                dve.wait_ge(y_taken, 4 * (s - 1) + n + 1)
                                nc.vector.tensor_tensor(u[1 - q][m][:], u[1 - q][m][:], gate[1 - q][m], ALU.mult
                                                        ).then_inc(y_full, 1)
                        if alive(i - 2):
                            if after(i - 2, 1):
                                dve.wait_ge(z_turned, 2 * (s - 2))
                            for k in range(TS):
                                dve.wait_ge(z_rstd, 2 * (s - 2) + k // 2 + 1)
                                nc.vector.tensor_scalar(zn[:, k, :], z[k // 2][:, k % 2, :], zmv[:, k, 0:1],
                                                        zrstd[:, k:k + 1], ALU.subtract, ALU.mult
                                                        ).then_inc(z_normed, 1)
                        if alive(i):
                            conv(2), conv(3)
                        if alive(i + 1):
                            if alive(i - 1):
                                dve.wait_ge(residual_in, s)
                            split_x(i + 1, 1 - q, s + 1)
                        if alive(i - 1):
                            for k in range(TS):
                                dve.wait_ge(z_done, 2 * (s - 1) + k // 2 + 1)
                                nc.vector.bn_stats(zstat[:, k, :], z[k // 2][:, k % 2, :]).then_inc(z_stat, 1)
                                dve.wait_ge(consts_made, 5)
                                dve.wait_ge(z_stat, 4 * (s - 1) + k + 1)
                                nc.vector.bn_aggr(zmv[:, k, :], zstat[:, k, :]).then_inc(z_mv, 1)
                                if k % 2:
                                    dve.wait_ge(z_mv, 4 * (s - 1) + k + 1)
                                    nc.vector.tensor_scalar(zvar[:, k - 1:k + 1], zmv[:, k - 1:k + 1, 1], EPS, None,
                                                            ALU.add).then_inc(z_var, 1)
                        if alive(i):
                            dve.wait_ge(bu_done, s + 1)
                            nc.vector.tensor_tensor_scan(hs[:], decay[:], bu[:], 0.0, ALU.mult, ALU.add
                                                         ).then_inc(scanned, 1)
                            dve.wait_ge(scanned, s + 1)
                            nc.vector.tensor_copy(hs_h[:], hs[:]).then_inc(hs_high, 1)
                            dve.wait_ge(hs_high, s + 1)
                            nc.vector.tensor_tensor(hs_l[:], hs[:], hs_h[:].bitcast(F32), ALU.subtract
                                                    ).then_inc(hs_low, 1)

                    pipeline(dve, body)

            @block.tensor
            def _(pe):
                pe.wait_ge(consts_made, 5)
                def turn_rows(r):
                    for j in range(SLOTS):
                        pair = j // 2
                        pe.wait_ge(pos_added, r * SLOTS + j + 1)
                        if j % 2 == 0 and (after(r, 1) or pair >= 2):
                            pe.wait_ge(x_ready, (SLOTS // 2) * r + pair - 1)
                        for k in range(KC):
                            last = nc.tensor.transpose(
                                proj[pair % 2][:, k * 2 * T + (j % 2) * T:k * 2 * T + (j % 2) * T + T],
                                emb[:, j, k * P:(k + 1) * P], ident[:])
                        if j % 2:
                            last.then_inc(emb_turned, 1)

                turn_rows(0)
                with pe.Fori(1, SEQS // SLOTS) as r:
                    turn_rows(r)

                with pe.Fori(0, LAYERS) as layer:
                    def body(i, q):
                        s = layer * G + i

                        def in_unit(m, is_gate):
                            bank = proj[2 * (m % 2) + is_gate]
                            if m < 2:
                                if after(i, 1):
                                    if is_gate:
                                        pe.wait_ge(gated, 4 * (s - 1) + m + 3)
                                    else:
                                        pe.wait_ge(conv_tap, 12 * (s - 1) + 3 * (m + 2) + 3)
                            elif after(i, 1):
                                pe.wait_ge(y_taken, 4 * (s - 1) + Y_ORDER.index(2 * (m - 2) + is_gate) + 1)
                            elif is_gate:
                                pe.wait_ge(gated, 4 * s + m - 1)
                            else:
                                pe.wait_ge(conv_tap, 12 * s + 3 * (m - 2) + 3)
                            c = is_gate * INNER + m * P
                            n = 0
                            for w, x in ((win_h, xh), (win_h, xl), (win_l, xh)):
                                for k in range(KC):
                                    last = nc.tensor.matmul(bank[:], w[:, k, c:c + P], x[q][:, k, :],
                                                            start=(n == 0), stop=(n == 5))
                                    n += 1
                            last.then_inc(in_proj, 1)

                        if alive(i):
                            pe.wait_ge(w_split, 4 * layer + 4)
                            pe.wait_ge(x_low, s + 1)
                            for m, is_gate in IN_ORDER[:4]:
                                in_unit(m, is_gate)
                        if alive(i - 1):
                            pe.wait_ge(hs_low, s)
                            for m in Y_ORDER:
                                if alive(i):
                                    if m % 2:
                                        pe.wait_ge(gated, 4 * s + m // 2 + 1)
                                    else:
                                        pe.wait_ge(conv_tap, 12 * s + 3 * (m // 2) + 3)
                                for n, (w, h) in enumerate(((wc_h, hs_h), (wc_h, hs_l), (wc_l, hs_h))):
                                    last = nc.tensor.matmul(proj[m][:], w[:, m * P:(m + 1) * P], h[:],
                                                            start=(n == 0), stop=(n == 2))
                                last.then_inc(hc_done, 1)
                        if alive(i):
                            for m, is_gate in IN_ORDER[4:]:
                                in_unit(m, is_gate)
                        def turn_back(k):
                            pe.wait_ge(z_normed, 4 * (s - 1))
                            if k:
                                pe.wait_ge(x_ready, 2 * G + 2 * (s - 2) + k)
                            elif after(i - 2, 1):
                                pe.wait_ge(x_ready, 2 * G + 2 * (s - 2))
                            for j in range(TS):
                                last = nc.tensor.transpose(zt[:, j * P:(j + 1) * P], zn[:, j, k * P:(k + 1) * P],
                                                           ident[:])
                            last.then_inc(z_turned, 1)

                        if alive(i - 2):
                            turn_back(0)
                        if alive(i - 1):
                            if after(i - 1, 1):
                                pe.wait_ge(z_normed, 4 * (s - 1))
                            for j in range(TS):
                                for k in range(KC):
                                    for n, x in enumerate((xh, xl)):
                                        last = nc.tensor.matmul(
                                            z[j // 2][:, j % 2, k * P:(k + 1) * P], x[1 - q][:, k, j * P:(j + 1) * P],
                                            ident_r[:], start=(j % 2 == 0 and k == 0 and n == 0), stop=False,
                                            skip_group_check=True)
                            last.then_inc(residual_in, 1)
                        if alive(i - 1):
                            pe.wait_ge(y_low, 4 * s)
                            for j in range(TS):
                                for m in range(MC):
                                    for n, (a, w) in enumerate(((yh, wo_h), (yh, wo_l), (yl, wo_h))):
                                        last = nc.tensor.matmul(
                                            z[j // 2][:, j % 2, :], a[:, m, j * P:(j + 1) * P], w[:, m, :],
                                            start=False, stop=(m == MC - 1 and n == 2), skip_group_check=True)
                                if j % 2:
                                    last.then_inc(z_done, 1)
                        if alive(i - 2):
                            turn_back(1)
                        if alive(i):
                            if after(i, 1):
                                pe.wait_ge(scanned, s)
                            for m in range(MC):
                                pe.wait_ge(u_low, 4 * s + m + 1)
                                nc.tensor.matmul(bu[:], wb_hl[:, m, :], uh[:, m, :], start=(m == 0), stop=False)
                                last = nc.tensor.matmul(bu[:], wb_hl[:, m, :], ul[:, m, :], start=False,
                                                        stop=(m == MC - 1))
                            last.then_inc(bu_done, 1)

                    pipeline(pe, body)


def attention_block(nc, t, x_res, ident, out, dims):
    SEQS, T, D, HEADS, TABLES, BITS = dims
    HD = D // HEADS
    R = 1 << BITS
    S = TABLES * R
    KC = D // P
    HC = 4
    HQ = HEADS // HC
    W = P // HQ
    UNROLL = 4

    with ExitStack() as ctx:
        def sb(name, shape, dt=F32):
            return ctx.enter_context(nc.sbuf_tensor(name, shape, dt))

        def two(name, shape, dt=F32):
            return [sb(f"{name}{i}", shape, dt) for i in range(2)]

        def ps(name, shape, dt=F32):
            return ctx.enter_context(nc.psum_tensor(name, shape, dt))

        def sem(name):
            return ctx.enter_context(nc.semaphore(name))

        e2 = two("e2", [P, HQ, HC, S])
        raw, wkv_raw = (tile[:, 0:2].rearrange("p (k a) c s -> p k (a c s)", k=KC) for tile in e2)
        wq_h, wq_l = sb("wq_h", [P, KC, HEADS * W], F32R), sb("wq_l", [P, KC, HEADS * W], F32R)
        wkv_h, wkv_l = sb("wkv_h", [P, KC, HEADS * W], F32R), sb("wkv_l", [P, KC, HEADS * W], F32R)
        wp_h, wp_l = sb("wp_h", [P, KC, HEADS * W], F32R), sb("wp_l", [P, KC, HEADS * W], F32R)
        protos = sb("protos", [P, HQ * S])
        planes = sb("planes", [P, P // HD * W])
        wo_h, wo_l = sb("awo_h", [P, HC, D], F32R), sb("awo_l", [P, HC, D], F32R)
        wf_h, wf_l = sb("wf_h", [P, KC, D], F32R), sb("wf_l", [P, KC, D], F32R)
        bo = sb("bo", [P, D])
        bias = sb("bias", [P, D])
        scal = sb("scal", [P, 8])
        half_neg = sb("ahalf_neg", [P, 1])
        xs = two("xs", [P, KC, T])
        stat, mv, var, rstd = sb("stat", [P, 6]), sb("mv", [P, 2]), sb("var", [P, 1]), sb("rstd", [P, 1])
        nt = two("nt", [P, D])
        nh, nl = sb("nh", [P, KC, 2, T], F32R), sb("nl", [P, KC, 2, T], F32R)
        th = sb("th", [P, 2, HC, T])
        qp = sb("qp", [P, UNROLL, HC, T])
        kv = sb("kv", [P, UNROLL, HEADS * W])
        lmax = sb("lmax", [P, HC, HQ * TABLES])
        e = two("e", [P, HC, HQ * S])
        lsum = sb("lsum", [P, HC, HQ * TABLES])
        lrec = two("lrec", [P, HC, HQ * TABLES])
        bkt = sb("bkt", [P, HC, S])
        bkv = two("bkv", [P, HEADS * W])
        nmx = sb("nmx", [P, HQ, HC])
        ssum = sb("ssum", [P, HQ, HC])
        srec = sb("srec", [P, HQ, HC])
        pe_t = sb("pe_t", [P, HQ, HC, T])
        wo_raw = pe_t[:, 0:2].rearrange("p a c t -> p (a c t)").rearrange("p (c d) -> p c d", d=D)
        oh, ol = sb("oh", [P, HC, T], F32R), sb("ol", [P, HC, T], F32R)
        wk_rows = pe_t[:, 2:3].rearrange("p a c t -> p (a c t)").rearrange("p (k d) -> p k d", d=D)
        wf_raw = pe_t[:, 3:4].rearrange("p a c t -> p (a c t)").rearrange("p (k d) -> p k d", d=D)
        xb = two("xb", [P, KC, T])
        h = sb("h", [P, D])
        hb = sb("hb", [P, D])
        stat2, mv2, var2, rstd2 = sb("stat2", [P, 6]), sb("mv2", [P, 2]), sb("var2", [P, 1]), sb("rstd2", [P, 1])
        v = sb("v", [P, D])
        ulp = sb("ulp", [P, D])
        qv = sb("qv", [P, D])
        qt = sb("qt", [P, KC, T], F32R)
        res = two("res", [P, D])

        big = [ps(f"big{i}", [P, 512]) for i in range(4)]
        rows_bank, even_bank, odd_bank, back_bank = (
            ps(name, [P, 512]) for name in ("rows_bank", "even_bank", "odd_bank", "back_bank"))

        names = """loaded zeroed made scales blocks raw_high w_done wp_in
            xs_copied x_turned stat_in mv_in var_in rstd_in n_in n_turned n_high n_low
            proj_done th_in q_done qp_in kv_done kv_in logits_in lmax_in shifted e_in lsum_in lrec_in p_in
            bucket_in bkt_in bkv_turned bkv_in s_in smax_in es_in srec_in share_in
            es_turned et_in o_in o_high o_low
            xb_copied y_in h_in hb_in stat2_in mv2_in var2_in rstd2_in quant q_turned qt_in f_in res_in""".split()
        sg = {n: sem("a_" + n) for n in names}
        out_sent = [sem(f"out_sent{i}") for i in range(2)]

        def alive(b):
            return not isinstance(b, int) or 0 <= b < SEQS

        def pipeline(eng, body):
            for i in range(-3, UNROLL):
                body(i, i % UNROLL)
            with eng.Fori(1, SEQS // UNROLL - 1) as quad:
                for u in range(UNROLL):
                    body(UNROLL * quad + u, u)
            for i in range(SEQS - UNROLL, SEQS + 4):
                body(i, i % UNROLL)

        with nc.Block() as block:

            @block.sync
            def _(sp):
                sp.dma_start(raw[:], t["wq"]).then_inc(sg["loaded"], 16)
                sp.dma_start(wkv_raw[:], t["wkv"]).then_inc(sg["loaded"], 16)
                sp.dma_start(wk_rows[:], t["wk_rows"]).then_inc(sg["loaded"], 16)
                sp.dma_start(wo_raw[:], t["wo_attn"]).then_inc(sg["loaded"], 16)
                sp.dma_start(wf_raw[:], t["wf"]).then_inc(sg["loaded"], 16)
                for tile, name in ((bo, "bo"), (bias, "bias")):
                    sp.dma_start(tile[:], t[name].partition_broadcast(P)).then_inc(sg["loaded"], 16)
                for c, name in enumerate(("logit_temp", "input_scale", "weight_scale")):
                    sp.dma_start(scal[:, c:c + 1], t[name].partition_broadcast(P)).then_inc(sg["loaded"], 16)
                sp.wait_ge(sg["zeroed"], 2)
                for j in range(P // HD):
                    sp.dma_start(planes[j * HD:(j + 1) * HD, j * W:(j + 1) * W], t["planes"]).then_inc(sg["blocks"], 16)
                for j in range(HQ * TABLES):
                    sp.dma_start(protos[j * BITS:(j + 1) * BITS, j * R:(j + 1) * R], t["protos"]
                                 ).then_inc(sg["blocks"], 16)

                def body(i, u):
                    b, q = i - 4, u % 2
                    if alive(b):
                        sp.wait_ge(sg["res_in"], b + 1)
                        sp.dma_start(out[bass.ds(b, 1), :, :].rearrange("b t d -> t (b d)"), res[q][:]
                                     ).then_inc(out_sent[q], 16)
                pipeline(sp, body)
                for q in range(2):
                    sp.wait_ge(out_sent[q], 16 * (SEQS // 2))

            @block.gpsimd
            def _(pool):
                nc.gpsimd.memset(planes[:], 0.0).then_inc(sg["zeroed"], 1)
                nc.gpsimd.memset(protos[:], 0.0).then_inc(sg["zeroed"], 1)
                nc.gpsimd.memset(half_neg[:], -0.5).then_inc(sg["made"], 1)
                pool.wait_ge(sg["made"], 1)
                pool.wait_ge(sg["loaded"], 160)

                def copy_rows(b, q):
                    if after(b, 2):
                        pool.wait_ge(sg["x_turned"], b - 1)
                    nc.gpsimd.tensor_copy(xs[q][:], x_res[:, :, bass.ds(b * T, T)]).then_inc(sg["xs_copied"], 1)

                copy_rows(0, 0)

                def body(i, u):
                    q = u % 2
                    if alive(i - 2):
                        pool.wait_ge(sg["srec_in"], i - 1)
                        for j in range(HQ):
                            nc.gpsimd.tensor_tensor(e2[q][:, j], e2[q][:, j],
                                                    srec[:, j, :].unsqueeze(2).broadcast_to([P, HC, S]), ALU.mult
                                                    ).then_inc(sg["share_in"], 1)
                    def table_share(c):
                        pool.wait_ge(sg["lrec_in"], 2 * i + c // 2 + 1)
                        ev = e[q][:, c, :].rearrange("p (a r) -> p a r", r=R)
                        rv = lrec[q][:, c, :].unsqueeze(2).broadcast_to([P, HQ * TABLES, R])
                        nc.gpsimd.tensor_tensor(ev, ev, rv, ALU.mult).then_inc(sg["p_in"], 1)

                    if alive(i):
                        for c in range(HC):
                            table_share(c)
                    if alive(i + 3):
                        pool.wait_ge(sg["var_in"], i + 4)
                        nc.gpsimd.tensor_tensor(rstd[:], var[:], half_neg[:], ALU.pow).then_inc(sg["rstd_in"], 1)
                    if alive(i - 3):
                        b = i - 3
                        pool.wait_ge(sg["var2_in"], b + 1)
                        nc.gpsimd.tensor_tensor(rstd2[:], var2[:], half_neg[:], ALU.pow).then_inc(sg["rstd2_in"], 1)
                        pool.wait_ge(sg["h_in"], b + 1)
                        if after(b, 1):
                            pool.wait_ge(sg["res_in"], b)
                        nc.gpsimd.tensor_tensor(hb[:], h[:], bias[:], ALU.add).then_inc(sg["hb_in"], 1)
                    if alive(i - 2):
                        if after(i, 4):
                            pool.wait_ge(sg["y_in"], i - 3)
                        nc.gpsimd.tensor_copy(xb[q][:], x_res[:, :, bass.ds((i - 2) * T, T)]).then_inc(sg["xb_copied"], 1)
                    if alive(i + 4):
                        copy_rows(i + 4, q)

                pipeline(pool, body)

            @block.scalar
            def _(act):
                act.wait_ge(sg["loaded"], 160)
                nc.scalar.activation(scal[:, 3:4], scal[:, 0:1], ACT.Exp).then_inc(sg["raw_high"], 1)
                nc.scalar.activation(wq_h[:], raw[:], ACT.Identity, scale=HD ** -0.5).then_inc(sg["raw_high"], 1)
                nc.scalar.activation(wkv_h[:], wkv_raw[:], ACT.Copy).then_inc(sg["raw_high"], 1)
                nc.scalar.activation(wo_h[:], wo_raw[:], ACT.Copy).then_inc(sg["raw_high"], 1)
                act.wait_ge(sg["w_done"], 1)
                nc.scalar.activation(wf_h[:], wf_raw[:], ACT.Copy).then_inc(sg["raw_high"], 1)
                for k in range(KC):
                    act.wait_ge(sg["wp_in"], k + 1)
                    nc.scalar.activation(wp_h[:, k, :], big[k][:], ACT.Copy).then_inc(sg["raw_high"], 1)

                def body(i, u):
                    q, r = u % 2, 1 - u % 2
                    banks = (even_bank, odd_bank)
                    paired = u % 2 == 0 and alive(i)

                    def take_projections(half, done, tile, slots, func, taken, count):
                        act.wait_ge(sg[done], i + count)
                        nc.scalar.activation(tile[:, slots, 2 * half:2 * half + 2, :],
                                             banks[half][:].rearrange("p (c s t) -> p s c t", c=2, s=2), func
                                             ).then_inc(sg[taken], 1)

                    def exp_logits(c):
                        act.wait_ge(sg["shifted"], 4 * i + c + 1)
                        nc.scalar.activation(e[q][:, c, :], e[q][:, c, :], ACT.Exp).then_inc(sg["e_in"], 1)

                    def take_turned(j):
                        act.wait_ge(sg["es_turned"], 4 * (i - 2) + j + 1)
                        nc.scalar.activation(pe_t[:, j], banks[1 - j % 2][:].rearrange("p (c t) -> p c t", c=HC),
                                             ACT.Copy).then_inc(sg["et_in"], 1)

                    def exp_scores(j, b=i - 1, slot=r):
                        act.wait_ge(sg["smax_in"], 4 * b + j + 1)
                        for c in range(HC):
                            last = nc.scalar.activation(e2[slot][:, j, c, :], big[j][:, c * S:(c + 1) * S], ACT.Exp,
                                                        bias=nmx[:, j, c:c + 1], accum_out=ssum[:, j, c:c + 1])
                        last.then_inc(sg["es_in"], 1)

                    if paired:
                        take_projections(0, "proj_done", th, slice(0, 2), ACT.Tanh, "th_in", 1)
                    if q == 0 and alive(i - 2):
                        exp_scores(3, i - 2, q)
                    if paired:
                        take_projections(1, "proj_done", th, slice(0, 2), ACT.Tanh, "th_in", 2)
                    if alive(i - 1):
                        act.wait_ge(sg["bucket_in"], i)
                        nc.scalar.activation(bkt[:], even_bank[:].rearrange("p (c s) -> p c s", c=HC), ACT.Copy
                                             ).then_inc(sg["bkt_in"], 1)
                    if alive(i - 1):
                        act.wait_ge(sg["bkv_turned"], i)
                        nc.scalar.activation(bkv[r][:], even_bank[:], ACT.Copy).then_inc(sg["bkv_in"], 1)
                    if alive(i - 4):
                        act.wait_ge(sg["q_turned"], i - 3)
                        nc.scalar.activation(qt[:], back_bank[:, 0:D].rearrange("p (k t) -> p k t", k=KC), ACT.Copy
                                             ).then_inc(sg["qt_in"], 1)
                    def take_norms():
                        if alive(i + 2):
                            act.wait_ge(sg["n_turned"], i + 3)
                            nc.scalar.activation(nh[:, :, q, :],
                                                 rows_bank[:, D:2 * D].rearrange("p (k t) -> p k t", k=KC),
                                                 ACT.Copy).then_inc(sg["n_high"], 1)

                    if paired:
                        exp_logits(0), exp_logits(1), exp_logits(2)
                        take_projections(1, "q_done", qp, slice(u, u + 2), ACT.Copy, "qp_in", 1)
                        exp_logits(3)
                        take_projections(0, "q_done", qp, slice(u, u + 2), ACT.Copy, "qp_in", 2)
                        for s in range(2):
                            act.wait_ge(sg["kv_done"], i + s + 1)
                            nc.scalar.activation(kv[:, u + s, :], banks[1 - s][:], ACT.Copy).then_inc(sg["kv_in"], 1)
                        take_norms()
                        if alive(i - 2):
                            take_turned(0), take_turned(1), take_turned(2), take_turned(3)
                    else:
                        if alive(i):
                            exp_logits(0), exp_logits(1)
                        take_norms()
                        if alive(i - 2):
                            take_turned(0)
                        if alive(i):
                            exp_logits(2)
                        if alive(i - 2):
                            take_turned(1)
                        if alive(i):
                            exp_logits(3)
                        if alive(i - 2):
                            take_turned(2), take_turned(3)
                    if alive(i - 1):
                        exp_scores(0), exp_scores(1)
                    if alive(i - 2):
                        act.wait_ge(sg["o_in"], i - 1)
                        nc.scalar.activation(oh[:], odd_bank[:].rearrange("p (c t) -> p c t", c=HC), ACT.Copy
                                             ).then_inc(sg["o_high"], 1)
                    if alive(i - 1):
                        exp_scores(2)
                        if q == 0:
                            exp_scores(3)

                pipeline(act, body)

            @block.vector
            def _(dve):
                dve.wait_ge(sg["raw_high"], 1)
                nc.vector.tensor_scalar(scal[:, 3:4], scal[:, 3:4], 0.01, 20.0, ALU.max, ALU.min).then_inc(sg["scales"], 1)
                nc.vector.tensor_tensor(scal[:, 5:6], scal[:, 1:2], scal[:, 2:3], ALU.mult).then_inc(sg["scales"], 1)
                nc.vector.reciprocal(scal[:, 6:7], scal[:, 1:2]).then_inc(sg["scales"], 1)
                dve.wait_ge(sg["scales"], 3)
                nc.vector.reciprocal(scal[:, 4:5], scal[:, 3:4]).then_inc(sg["scales"], 1)
                nc.vector.tensor_scalar(wf_raw[:], wf_raw[:], scal[:, 5:6], None, ALU.mult).then_inc(sg["w_done"], 1)
                dve.wait_ge(sg["scales"], 4)
                dve.wait_ge(sg["blocks"], 16 * (P // HD + HQ * TABLES))
                nc.vector.tensor_scalar(protos[:], protos[:], scal[:, 4:5], None, ALU.mult).then_inc(sg["w_done"], 1)
                dve.wait_ge(sg["raw_high"], 7)
                dve.wait_ge(sg["w_done"], 2)
                nc.vector.scalar_tensor_tensor(wq_l[:], raw[:], HD ** -0.5, wq_h[:].bitcast(F32), ALU.mult, ALU.subtract
                                               ).then_inc(sg["w_done"], 1)
                for lo, full, hi in ((wkv_l, wkv_raw, wkv_h), (wo_l, wo_raw, wo_h), (wf_l, wf_raw, wf_h)):
                    nc.vector.tensor_tensor(lo[:], full[:], hi[:].bitcast(F32), ALU.subtract).then_inc(sg["w_done"], 1)
                for k in range(KC):
                    nc.vector.tensor_tensor(wp_l[:, k, :], big[k][:], wp_h[:, k, :].bitcast(F32), ALU.subtract
                                            ).then_inc(sg["w_done"], 1)

                def body(i, u):
                    q = u % 2

                    def most_logits(c):
                        dve.wait_ge(sg["logits_in"], 4 * i + c + 1)
                        nc.vector.tensor_reduce(lmax[:, c, :], big[c][:].rearrange("p (a r) -> p a r", r=R), AX.X,
                                                ALU.max).then_inc(sg["lmax_in"], 1)

                    def shift(c):
                        dve.wait_ge(sg["lmax_in"], 4 * i + c + 1)
                        nc.vector.tensor_tensor(e[q][:, c, :].rearrange("p (a r) -> p a r", r=R),
                                                big[c][:].rearrange("p (a r) -> p a r", r=R),
                                                lmax[:, c, :].unsqueeze(2).broadcast_to([P, HQ * TABLES, R]),
                                                ALU.subtract).then_inc(sg["shifted"], 1)

                    def total(half):
                        dve.wait_ge(sg["e_in"], 4 * i + 2 * half + 2)
                        nc.vector.tensor_reduce(lsum[:, 2 * half:2 * half + 2, :],
                                                e[q][:, 2 * half:2 * half + 2, :].rearrange("p c (a r) -> p c a r", r=R),
                                                AX.X, ALU.add).then_inc(sg["lsum_in"], 1)

                    def total_reciprocal(half):
                        dve.wait_ge(sg["lsum_in"], 2 * i + half + 1)
                        nc.vector.reciprocal(lrec[q][:, 2 * half:2 * half + 2, :], lsum[:, 2 * half:2 * half + 2, :]
                                             ).then_inc(sg["lrec_in"], 1)

                    def most(j):
                        dve.wait_ge(sg["s_in"], 4 * (i - 1) + j + 1)
                        nc.vector.tensor_reduce(nmx[:, j, :], big[j][:].rearrange("p (c s) -> p c s", c=HC),
                                                AX.X, ALU.max, negate=True).then_inc(sg["smax_in"], 1)

                    def rounding(step):
                        b = i - 3
                        if step:
                            dve.wait_ge(sg["quant"], 7 * b + step)
                        else:
                            dve.wait_ge(sg["rstd2_in"], b + 1)
                            ins = nc.vector.tensor_scalar(v[:], h[:], mv2[:, 0:1], rstd2[:, 0:1], ALU.subtract, ALU.mult)
                        if step == 1:
                            ins = nc.vector.tensor_scalar(v[:], v[:], scal[:, 6:7], FP8_MAX, ALU.mult, ALU.min)
                        elif step == 2:
                            ins = nc.vector.tensor_scalar(v[:], v[:], -FP8_MAX, None, ALU.max)
                        elif step == 3:
                            ins = nc.vector.tensor_scalar(ulp[:].bitcast(U32), v[:].bitcast(U32), 0x7F800000, None,
                                                          ALU.bitwise_and)
                        elif step == 4:
                            ins = nc.vector.tensor_scalar(ulp[:], ulp[:], 2.0 ** -6, 1.5 * 2.0 ** 20, ALU.max, ALU.mult)
                        elif step == 5:
                            ins = nc.vector.tensor_tensor(v[:], v[:], ulp[:], ALU.add)
                        elif step == 6:
                            if after(b, 1):
                                dve.wait_ge(sg["q_turned"], b)
                            ins = nc.vector.tensor_tensor(qv[:], v[:], ulp[:], ALU.subtract)
                        ins.then_inc(sg["quant"], 1)

                    def finish_rows():
                        b = i - 4
                        dve.wait_ge(sg["f_in"], b + 1)
                        dve.wait_ge(sg["hb_in"], b + 1)
                        if after(b, 2):
                            dve.wait_ge(out_sent[q], 8 * (b - q))
                        nc.vector.tensor_tensor(res[q][:], back_bank[:, D:2 * D], hb[:], ALU.add).then_inc(sg["res_in"], 1)

                    if alive(i - 2):
                        dve.wait_ge(sg["es_in"], 4 * (i - 2) + 4)
                        nc.vector.reciprocal(srec[:], ssum[:]).then_inc(sg["srec_in"], 1)
                    if alive(i):
                        most_logits(0), most_logits(1), shift(0), most_logits(2), shift(1), most_logits(3), shift(2)
                    if q == 1 and alive(i - 4):
                        finish_rows()
                    if alive(i):
                        shift(3)
                    if q == 0 and alive(i - 4):
                        finish_rows()
                    if alive(i):
                        total(0)
                    if alive(i):
                        total_reciprocal(0)
                    if alive(i):
                        total(1)
                    if alive(i + 2):
                        dve.wait_ge(sg["n_high"], i + 3)
                        nc.vector.tensor_tensor(nl[:, :, q, :], rows_bank[:, D:2 * D].rearrange("p (k t) -> p k t", k=KC),
                                                nh[:, :, q, :].bitcast(F32), ALU.subtract).then_inc(sg["n_low"], 1)
                    if alive(i):
                        total_reciprocal(1)
                    if alive(i - 1):
                        most(0), most(1)
                    if alive(i - 3):
                        b = i - 3
                        dve.wait_ge(sg["y_in"], b + 1)
                        if after(b, 1):
                            dve.wait_ge(sg["hb_in"], b)
                        nc.vector.tensor_tensor(h[:], back_bank[:, D:2 * D], bo[:], ALU.add).then_inc(sg["h_in"], 1)
                    if alive(i - 1):
                        most(2)
                    if alive(i - 1):
                        most(3)
                    if alive(i + 3):
                        dve.wait_ge(sg["x_turned"], i + 4)
                        nc.vector.bn_stats(stat[:], rows_bank[:, 0:D]).then_inc(sg["stat_in"], 1)
                    if alive(i - 3):
                        dve.wait_ge(sg["h_in"], b + 1)
                        nc.vector.bn_stats(stat2[:], h[:]).then_inc(sg["stat2_in"], 1)
                    if alive(i + 3):
                        dve.wait_ge(sg["w_done"], 2)
                        dve.wait_ge(sg["stat_in"], i + 4)
                        nc.vector.bn_aggr(mv[:], stat[:]).then_inc(sg["mv_in"], 1)
                    if alive(i + 3):
                        dve.wait_ge(sg["mv_in"], i + 4)
                        nc.vector.tensor_scalar(var[:], mv[:, 1:2], EPS, None, ALU.add).then_inc(sg["var_in"], 1)
                    if alive(i - 3):
                        dve.wait_ge(sg["w_done"], 2)
                        dve.wait_ge(sg["stat2_in"], b + 1)
                        nc.vector.bn_aggr(mv2[:], stat2[:]).then_inc(sg["mv2_in"], 1)
                        dve.wait_ge(sg["mv2_in"], b + 1)
                        nc.vector.tensor_scalar(var2[:], mv2[:, 1:2], EPS, None, ALU.add).then_inc(sg["var2_in"], 1)
                    if alive(i - 2):
                        dve.wait_ge(sg["o_high"], i - 1)
                        nc.vector.tensor_tensor(ol[:], odd_bank[:].rearrange("p (c t) -> p c t", c=HC),
                                                oh[:].bitcast(F32), ALU.subtract).then_inc(sg["o_low"], 1)
                    if alive(i + 3):
                        dve.wait_ge(sg["rstd_in"], i + 4)
                        nc.vector.tensor_scalar(nt[1 - q][:], rows_bank[:, 0:D], mv[:, 0:1], rstd[:, 0:1], ALU.subtract,
                                                ALU.mult).then_inc(sg["n_in"], 1)
                    if alive(i - 3):
                        for step in range(7):
                            rounding(step)

                pipeline(dve, body)

            @block.tensor
            def _(pe):
                pe.wait_ge(sg["loaded"], 160)
                pe.wait_ge(sg["blocks"], 16 * (P // HD + HQ * TABLES))
                for k in range(KC):
                    for c in range(KC):
                        last = nc.tensor.matmul(big[k][:, c * 256:(c + 1) * 256], wk_rows[:, c, k * P:(k + 1) * P],
                                                planes[:], start=True, stop=True)
                    last.then_inc(sg["wp_in"], 1)
                pe.wait_ge(sg["w_done"], 8)

                def three(outp, high, low, rhs_high, rhs_low, chunks, final=True):
                    n = 0
                    for l, r in ((high, rhs_high), (high, rhs_low), (low, rhs_high)):
                        for k in range(chunks):
                            last = nc.tensor.matmul(outp, l(k), r(k), start=(n == 0),
                                                    stop=(final and n == 3 * chunks - 1), skip_group_check=True)
                            n += 1
                    return last

                def body(i, u):
                    q, r = u % 2, 1 - u % 2
                    banks = (even_bank, odd_bank)
                    paired = u % 2 == 0 and alive(i)

                    def projections(half, high, low):
                        for c in (2 * half, 2 * half + 1):
                            cut = slice(c * P, (c + 1) * P)
                            last = three(banks[half][:, c % 2 * 2 * T:(c % 2 + 1) * 2 * T],
                                         lambda k: high[:, k, cut], lambda k: low[:, k, cut],
                                         lambda k: nh[:, k].rearrange("p s t -> p (s t)"),
                                         lambda k: nl[:, k].rearrange("p s t -> p (s t)"), KC)
                        return last

                    if paired:
                        pe.wait_ge(sg["n_low"], i + 2)
                        if after(i, 2):
                            pe.wait_ge(sg["bkv_in"], i - 1)
                        projections(0, wp_h, wp_l).then_inc(sg["proj_done"], 1)
                        if after(i, 3):
                            pe.wait_ge(sg["o_low"], i - 2)
                        projections(1, wp_h, wp_l).then_inc(sg["proj_done"], 1)
                    if alive(i - 1):
                        b = i - 1
                        if paired:
                            pe.wait_ge(sg["th_in"], i + 1)
                        pe.wait_ge(sg["kv_in"], i + q)
                        for c in range(HC):
                            pe.wait_ge(sg["p_in"], 4 * b + c + 1)
                            for j in range(HQ):
                                hd = c * HQ + j
                                last = nc.tensor.matmul(even_bank[j * W:(j + 1) * W, c * S:(c + 1) * S],
                                                        kv[:, (u - 1) % UNROLL, hd * W:(hd + 1) * W],
                                                        e[r][:, c, j * S:(j + 1) * S], start=True, stop=True)
                        last.then_inc(sg["bucket_in"], 1)
                    def logits():
                        pe.wait_ge(sg["th_in"], i + 2 - q)
                        for c in range(HC):
                            if alive(i - 2):
                                pe.wait_ge(sg["es_in"], 4 * (i - 2) + c + 1)
                            elif i == 1:
                                pe.wait_ge(sg["shifted"], c + 1)
                            nc.tensor.matmul(big[c][:], th[:, q, c, :], protos[:], start=True, stop=True
                                             ).then_inc(sg["logits_in"], 1)

                    if alive(i):
                        logits()
                    if alive(i - 1):
                        pe.wait_ge(sg["bkt_in"], i)
                        for c in range(HC):
                            last = nc.tensor.transpose(even_bank[:, c * P:(c + 1) * P], bkt[:, c, :], ident[:])
                        last.then_inc(sg["bkv_turned"], 1)

                    if alive(i - 4):
                        b = i - 4
                        pe.wait_ge(sg["quant"], 7 * b + 7)
                        for k in range(KC):
                            last = nc.tensor.transpose(back_bank[:, k * P:(k + 1) * P], qv[:, k * P:(k + 1) * P],
                                                       ident[:])
                        last.then_inc(sg["q_turned"], 1)
                    def fp8_layer():
                        b = i - 4
                        pe.wait_ge(sg["qt_in"], b + 1)
                        n = 0
                        for w in (wf_h, wf_l):
                            for k in range(KC):
                                last = nc.tensor.matmul(back_bank[:, D:2 * D], qt[:, k, :], w[:, k, :], start=(n == 0),
                                                        stop=(n == 3))
                                n += 1
                        last.then_inc(sg["f_in"], 1)

                    if paired:
                        projections(1, wq_h, wq_l).then_inc(sg["q_done"], 1)
                        if alive(i - 4):
                            fp8_layer()
                        if alive(i - 1):
                            pe.wait_ge(sg["bkv_in"], i)
                        projections(0, wq_h, wq_l).then_inc(sg["q_done"], 1)
                        for s in range(2):
                            pe.wait_ge(sg["qp_in"], i + s + 1)
                            three(banks[1 - s][:], lambda k: nh[:, k, s, :], lambda k: nl[:, k, s, :],
                                  lambda k: wkv_h[:, k, :], lambda k: wkv_l[:, k, :], KC).then_inc(sg["kv_done"], 1)
                    if alive(i + 2):
                        pe.wait_ge(sg["n_in"], i + 3)
                        for k in range(KC):
                            last = nc.tensor.transpose(rows_bank[:, D + k * P:D + (k + 1) * P],
                                                       nt[q][:, k * P:(k + 1) * P], ident[:])
                        last.then_inc(sg["n_turned"], 1)
                    def turn_scores(j):
                        b = i - 2
                        if j == 0:
                            if paired:
                                pe.wait_ge(sg["kv_in"], i + 1)
                            elif alive(i - 3):
                                pe.wait_ge(sg["o_low"], i - 2)
                        elif j == 1:
                            if paired:
                                pe.wait_ge(sg["kv_in"], i + 2)
                            elif alive(i - 1):
                                pe.wait_ge(sg["bkv_in"], i)
                        else:
                            pe.wait_ge(sg["et_in"], 4 * b + j - 1)
                        pe.wait_ge(sg["share_in"], 4 * b + j + 1)
                        for c in range(HC):
                            last = nc.tensor.transpose(banks[1 - j % 2][:, c * T:(c + 1) * T], e2[q][:, j, c, :],
                                                       ident[:])
                        last.then_inc(sg["es_turned"], 1)

                    def scores(pair):
                        for j in pair:
                            if alive(i):
                                pe.wait_ge(sg["shifted"], 4 * i + j + 1)
                            elif alive(i - 2):
                                pe.wait_ge(sg["es_in"], 4 * (i - 2) + j + 1)
                        for c in range(HC):
                            for j in pair:
                                last = nc.tensor.matmul(big[j][:, c * S:(c + 1) * S],
                                                        qp[j * W:(j + 1) * W, (u - 1) % UNROLL, c, :],
                                                        bkt[j * W:(j + 1) * W, c, :], start=True, stop=True)
                                if c == HC - 1:
                                    last.then_inc(sg["s_in"], 1)

                    if alive(i - 2):
                        turn_scores(0)
                    if alive(i - 4) and not paired:
                        fp8_layer()
                    if alive(i - 2):
                        turn_scores(1)
                    if alive(i - 1):
                        scores((0, 1))
                    if alive(i - 3):
                        b = i - 3
                        pe.wait_ge(sg["o_low"], b + 1)
                        if after(b, 1):
                            pe.wait_ge(sg["res_in"], b)
                        three(back_bank[:, D:2 * D], lambda k: oh[:, k, :], lambda k: ol[:, k, :],
                              lambda k: wo_h[:, k, :], lambda k: wo_l[:, k, :], HC, final=False)
                        pe.wait_ge(sg["xb_copied"], b + 1)
                        for k in range(KC):
                            last = nc.tensor.matmul(back_bank[:, D + k * P:D + (k + 1) * P], xb[r][:, k, :], ident[:],
                                                    start=False, stop=(k == KC - 1), skip_group_check=True)
                        last.then_inc(sg["y_in"], 1)
                    if alive(i - 2):
                        turn_scores(2), turn_scores(3)
                    if alive(i - 1):
                        scores((2, 3))
                    if alive(i + 3):
                        pe.wait_ge(sg["xs_copied"], i + 4)
                        if after(i + 3, 1):
                            pe.wait_ge(sg["n_low"], i + 3)
                        for k in range(KC):
                            last = nc.tensor.transpose(rows_bank[:, k * P:(k + 1) * P], xs[r][:, k, :], ident[:])
                        last.then_inc(sg["x_turned"], 1)
                    if alive(i - 2):
                        b = i - 2
                        for j in range(HQ):
                            pe.wait_ge(sg["et_in"], 4 * b + 4)
                            for c in range(HC):
                                hd = c * HQ + j
                                last = nc.tensor.matmul(odd_bank[j * W:(j + 1) * W, c * T:(c + 1) * T],
                                                        bkv[q][:, hd * W:(hd + 1) * W], pe_t[:, j, c, :],
                                                        start=True, stop=True)
                        last.then_inc(sg["o_in"], 1)

                pipeline(pe, body)


def build(nc, t, out, dims):
    SEQS, T, D, INNER, N, LAYERS, HEADS, TABLES, BITS = dims
    with ExitStack() as ctx:
        x_res = ctx.enter_context(nc.sbuf_tensor("x_res", [P, D // P, SEQS * T], F32))
        ident = ctx.enter_context(nc.sbuf_tensor("ident", [P, P], F32))
        tower_block(nc, t, x_res, ident, (SEQS, T, D, INNER, N, LAYERS))
        attention_block(nc, t, x_res, ident, out, (SEQS, T, D, HEADS, TABLES, BITS))


def kernel(**inputs):
    import numpy as np
    import concourse.bacc as bacc
    from concourse.bass_utils import run_bass_kernel_spmd

    a = {k.replace("L0_", ""): np.asarray(v) for k, v in inputs.items()}
    seqs, T = a["x"].shape
    layers, n, inner = a["tok_W_B"].shape
    d = a["tok_tok_emb"].shape[1]
    dim, heads = a["attn_planes_T"].shape[0], d // a["attn_planes_T"].shape[0]
    bits, protos = a["attn_protos_T"].shape
    tables = a["attn_planes_T"].shape[1] // bits
    mc, kc, w = inner // P, d // P, 32

    def rows(m):
        m = m.reshape(*m.shape[:-2], m.shape[-2] // P, P, m.shape[-1])
        return np.swapaxes(m, -3, -2)

    def per_channel(m):
        m = m.reshape(layers, -1, P, *m.shape[2:])
        return np.moveaxis(m, 2, 0).reshape(P, layers, -1)

    params = np.concatenate([per_channel(a["tok_conv_w"][:, :, 0, :]), per_channel(a["tok_conv_b"]),
                             per_channel(a["tok_D_vec"]), per_channel(a["tok_ln_g"]), per_channel(a["tok_ln_b"])], -1)
    wq = np.zeros((d, heads, w), np.float32)
    wq[:, :, :dim] = a["attn_Wq"].T.reshape(d, heads, dim)
    wo = np.zeros((heads, w, d), np.float32)
    wo[:, dim:] = a["attn_Wo"].T.reshape(heads, dim, d)
    wkv = np.concatenate([a["attn_Wk"].T.reshape(d, heads, dim), a["attn_Wv"].T.reshape(d, heads, dim)], -1)
    arrays = {
        "tokens": a["x"].T, "tok_emb": a["tok_tok_emb"], "pos_emb": a["tok_pos_emb"], "params": params,
        "win": rows(np.swapaxes(a["tok_W_in"], 1, 2)), "wb": rows(np.swapaxes(a["tok_W_B"], 1, 2)),
        "wc": np.swapaxes(a["tok_W_C"], 1, 2), "wo": rows(np.swapaxes(a["tok_W_out"], 1, 2)),
        "wq": rows(wq.reshape(d, heads * w)), "wkv": rows(wkv.reshape(d, heads * w)), "wk_rows": rows(a["attn_Wk"]),
        "wo_attn": rows(wo.reshape(heads * w, d)), "wf": rows(a["ffn_weight_fp8"].T), "bo": a["attn_bo"], "bias": a["ffn_bias"],
        "logit_temp": a["attn_logit_temp"].reshape(1), "input_scale": a["ffn_input_scale"],
        "weight_scale": a["ffn_weight_scale"], "planes": a["attn_planes_T"], "protos": a["attn_protos_T"],
    }
    nc = bacc.Bacc("TRN2", target_bir_lowering=False, num_devices=1)
    arrays = {f"in_{k}": np.ascontiguousarray(v) for k, v in arrays.items()}
    t = {k[3:]: nc.dram_tensor(k, v.shape, mybir.dt.from_np(v.dtype), kind="ExternalInput").ap()
         for k, v in arrays.items()}
    out = nc.dram_tensor("out", (seqs, T, d), F32, kind="ExternalOutput").ap()
    build(nc, t, out, (seqs, T, d, inner, n, layers, heads, tables, bits))
    r = run_bass_kernel_spmd(nc, [arrays], core_ids=[0])
    return r.results[0]["out"]
```
